# Optimizing a Trainium2 kernel written in Bass

```python
import numpy as np
import jax
import jax.numpy as jnp

def _softmax(x, axis=-1):
    return jax.nn.softmax(x, axis=axis)

def _gelu(x):
    return jax.nn.gelu(x, approximate=True)

def _silu(x):
    return jax.nn.silu(x)

def _sigmoid(x):
    return jax.nn.sigmoid(x)

def _layernorm(x, axis=-1, eps=1e-05):
    m = jnp.mean(x, axis=axis, keepdims=True)
    v = jnp.var(x, axis=axis, keepdims=True)
    return (x - m) / jnp.sqrt(v + eps)

def _scatter_add(tgt, idx, src, axis=0):
    return tgt.at[idx].add(src)

def _segment_sum(src, seg, n):
    return jax.ops.segment_sum(src, seg, n)
kernel_name = 'mk_flamingo_gated_d1_seqx_r8_98603e'

def setup_inputs(seed: int=0):
    np.random.seed(seed)
    _w = jnp.asarray

    def _rec_inputs():
        import jax
        import jax.numpy as jnp
        _rk = jax.random.key(seed)
        x = 7.22e-05 + 1 * jax.random.normal(jax.random.fold_in(_rk, 1), (4, 256, 128), jnp.float32)
        _lenS = 256 - jax.random.randint(jax.random.fold_in(_rk, 7), (4,), 0, max(1, 256 // 4) + 1, jnp.int32)
        _lenS2 = 256 - jax.random.randint(jax.random.fold_in(_rk, 8), (4,), 0, max(1, 256 // 4) + 1, jnp.int32)
        _ctx_1024P = jax.random.normal(jax.random.fold_in(_rk, 11), (4, 16, 128), jnp.float32)
        _ctx_1024c = jax.random.dirichlet(jax.random.fold_in(_rk, 511), 0.3 * jnp.ones((16,), jnp.float32), (4, 256))
        _ctx_1024t = jnp.einsum('bsk,bkd->bsd', _ctx_1024c, _ctx_1024P)
        _ctx_1024t = _ctx_1024t * jax.lax.rsqrt(jnp.mean(jnp.square(_ctx_1024t)) + 1e-12) * 0.953939
        ctx_1024 = 4.13588e-05 + 0.999923 * (_ctx_1024t + 0.3 * jax.random.normal(jax.random.fold_in(_rk, 611), (4, 256, 128), jnp.float32))
        _validS = jnp.arange(256)[None, :] < _lenS[:, None]
        _validS2 = jnp.arange(256)[None, :] < _lenS2[:, None]
        _causal = jnp.tril(jnp.ones((256, 256), dtype=bool))
        mask_BxS2_bf0 = jnp.logical_not(jnp.ones((4, 256), dtype=bool))
        _g = jax.random.normal(jax.random.fold_in(_rk, 9001), (2, 1), jnp.float32)
        _g = jnp.sign(_g) * jnp.maximum(jnp.abs(_g), 1.0) + (_g == 0) * 1.0
        g_xattn = _g[0]
        g_ffn = _g[1]
        return (x, ctx_1024, mask_BxS2_bf0, g_xattn, g_ffn)
    x, ctx_1024, mask_BxS2_bf0, g_xattn, g_ffn = _rec_inputs()

    def _L0_xattn_setup():
        import jax, jax.numpy as jnp
        import numpy as np
        DIM = 128
        N_HEAD = 16
        BS, QLEN, KLEN = (4, 256, 256)
        key = jax.random.key(seed)
        ks = jax.random.split(key, 12)
        s = 1.0 / np.sqrt(DIM)
        inp = {'q_in': jax.random.normal(ks[0], (BS, QLEN, DIM), jnp.float32), 'k_in': jax.random.normal(ks[1], (BS, KLEN, DIM), jnp.float32), 'v_in': jax.random.normal(ks[2], (BS, KLEN, DIM), jnp.float32), 'key_padding_mask': jnp.zeros((BS, KLEN), dtype=bool), 'Wq': jax.random.normal(ks[3], (DIM, DIM), jnp.float32) * s, 'bq': jnp.zeros((DIM,), jnp.float32), 'Wk': jax.random.normal(ks[4], (DIM, DIM), jnp.float32) * s, 'bk': jnp.zeros((DIM,), jnp.float32), 'Wv': jax.random.normal(ks[5], (DIM, DIM), jnp.float32) * s, 'bv': jnp.zeros((DIM,), jnp.float32), 'Wo': jax.random.normal(ks[6], (DIM, DIM), jnp.float32) * s, 'bo': jnp.zeros((DIM,), jnp.float32)}
        return inp
    _L0_xattn_all = _L0_xattn_setup()
    _L0_xattn_in = {k: v for k, v in _L0_xattn_all.items() if k in ('Wq', 'bq', 'Wk', 'bk', 'Wv', 'bv', 'Wo', 'bo')}
    del _L0_xattn_all

    def _L0_ffn_setup():
        import jax, jax.numpy as jnp
        import numpy as np
        DIM = 128
        DEPTH = 6
        HEADS = 16
        DIM_HEAD = 64
        WINDOW = 32
        INNER = HEADS * DIM_HEAD
        DIM_INNER = int(DIM * 4 * 2 / 3)
        QK_SCALE = 8.0

        def shift_tokens(t):
            a, s = jnp.split(t, 2, -1)
            s = jnp.pad(s, ((0, 0), (1, 0), (0, 0)))[:, :-1]
            return jnp.concatenate([a, s], -1)

        def l2norm(t):
            return t / jnp.maximum(jnp.linalg.norm(t, axis=-1, keepdims=True), 1e-12)

        def rotate_half(x):
            x1, x2 = jnp.split(x, 2, -1)
            return jnp.concatenate([-x2, x1], -1)

        def rotary_tables(n):
            half = jnp.arange(0, DIM_HEAD, 2, dtype=jnp.float32)
            inv_freq = 1.0 / 10000.0 ** (half / DIM_HEAD)
            t = jnp.arange(n, dtype=jnp.float32)
            freqs = t[:, None] * inv_freq[None, :]
            freqs = jnp.concatenate([freqs, freqs], -1)
            base_scale = (half + 0.4 * DIM_HEAD) / (1.4 * DIM_HEAD)
            power = (t - n // 2) / (WINDOW // 2)
            scale = base_scale[None, :] ** power[:, None]
            scale = jnp.concatenate([scale, scale], -1)
            return (freqs, scale)

        def local_attention(q, k, v):
            b, h, n, d = q.shape
            w = WINDOW
            nw = n // w
            bq = q.reshape(b, h, nw, w, d)
            bk = k.reshape(b, h, nw, w, d)
            bv = v.reshape(b, h, nw, w, d)

            def look(t):
                p = jnp.pad(t, ((0, 0), (0, 0), (1, 0), (0, 0), (0, 0)))
                return jnp.concatenate([p[:, :, :nw], p[:, :, 1:]], axis=3)
            bk2, bv2 = (look(bk), look(bv))
            seq = jnp.arange(n).reshape(nw, w)
            seq_p = jnp.pad(seq, ((1, 0), (0, 0)), constant_values=-1)
            jt = jnp.concatenate([seq_p[:nw], seq_p[1:]], axis=1)
            it = seq[:, :, None]
            jb = jt[:, None, :]
            mask = (it < jb) | (it > jb + w) | (jb == -1)
            sim = jnp.einsum('bhwie,bhwje->bhwij', bq, bk2) * QK_SCALE
            sim = jnp.where(mask, -jnp.finfo(sim.dtype).max, sim)
            attn = jax.nn.softmax(sim, -1)
            out = jnp.einsum('bhwij,bhwje->bhwie', attn, bv2)
            return out.reshape(b, h, n, d)

        def attn_layer(x, Wqkv, qs, ksc, Wo):
            b, n, _ = x.shape
            qkv = x @ Wqkv
            q, k, v = jnp.split(qkv, 3, -1)
            sh = lambda t: t.reshape(b, n, HEADS, DIM_HEAD).transpose(0, 2, 1, 3)
            q, k, v = (sh(q), sh(k), sh(v))
            q = l2norm(q) * qs
            k = l2norm(k) * ksc
            freqs, scale = rotary_tables(n)
            cos, sin = (jnp.cos(freqs), jnp.sin(freqs))
            q = q * cos * scale + rotate_half(q) * sin * scale
            inv = 1.0 / scale
            k = k * cos * inv + rotate_half(k) * sin * inv
            out = local_attention(q, k, v)
            out = out.transpose(0, 2, 1, 3).reshape(b, n, INNER)
            return out @ Wo

        def ffn_layer(x, g, bln, W1, b1, W2, b2):
            mu = x.mean(-1, keepdims=True)
            var = ((x - mu) ** 2).mean(-1, keepdims=True)
            xn = (x - mu) / jnp.sqrt(var + 1e-05) * g + bln
            hg = xn @ W1 + b1
            a, gate = jnp.split(hg, 2, -1)
            return a * jax.nn.gelu(gate, approximate=False) @ W2 + b2
        key = jax.random.key(seed)
        ks = jax.random.split(key, 8)
        B, N = (2, 256)
        init = lambda k, shape: jax.random.normal(k, shape, jnp.float32) * 0.02
        return {'x': jax.random.normal(ks[0], (B, N, DIM), jnp.float32), 'Wqkv': init(ks[1], (DEPTH, DIM, 3 * INNER)), 'q_scale': jnp.ones((DEPTH, DIM_HEAD), jnp.float32), 'k_scale': jnp.ones((DEPTH, DIM_HEAD), jnp.float32), 'Wo': init(ks[2], (DEPTH, INNER, DIM)), 'ln_g': jnp.ones((DEPTH, DIM), jnp.float32), 'ln_b': jnp.zeros((DEPTH, DIM), jnp.float32), 'W1': init(ks[3], (DEPTH, DIM, 2 * DIM_INNER)), 'b1': jnp.zeros((DEPTH, 2 * DIM_INNER), jnp.float32), 'W2': init(ks[4], (DEPTH, DIM_INNER, DIM)), 'b2': jnp.zeros((DEPTH, DIM), jnp.float32)}
    _L0_ffn_all = _L0_ffn_setup()
    _L0_ffn_in = {k: v for k, v in _L0_ffn_all.items() if k in ('Wqkv', 'q_scale', 'k_scale', 'Wo', 'ln_g', 'ln_b', 'W1', 'b1', 'W2', 'b2')}
    del _L0_ffn_all
    return {'x': x, 'ctx_1024': ctx_1024, 'mask_BxS2_bf0': mask_BxS2_bf0, 'g_xattn': g_xattn, 'g_ffn': g_ffn, 'L0_xattn_Wq': _L0_xattn_in['Wq'], 'L0_xattn_bq': _L0_xattn_in['bq'], 'L0_xattn_Wk': _L0_xattn_in['Wk'], 'L0_xattn_bk': _L0_xattn_in['bk'], 'L0_xattn_Wv': _L0_xattn_in['Wv'], 'L0_xattn_bv': _L0_xattn_in['bv'], 'L0_xattn_Wo': _L0_xattn_in['Wo'], 'L0_xattn_bo': _L0_xattn_in['bo'], 'L0_ffn_Wqkv': _L0_ffn_in['Wqkv'], 'L0_ffn_q_scale': _L0_ffn_in['q_scale'], 'L0_ffn_k_scale': _L0_ffn_in['k_scale'], 'L0_ffn_Wo': _L0_ffn_in['Wo'], 'L0_ffn_ln_g': _L0_ffn_in['ln_g'], 'L0_ffn_ln_b': _L0_ffn_in['ln_b'], 'L0_ffn_W1': _L0_ffn_in['W1'], 'L0_ffn_b1': _L0_ffn_in['b1'], 'L0_ffn_W2': _L0_ffn_in['W2'], 'L0_ffn_b2': _L0_ffn_in['b2']}

def reference(x, ctx_1024, mask_BxS2_bf0, g_xattn, g_ffn, L0_xattn_Wq, L0_xattn_bq, L0_xattn_Wk, L0_xattn_bk, L0_xattn_Wv, L0_xattn_bv, L0_xattn_Wo, L0_xattn_bo, L0_ffn_Wqkv, L0_ffn_q_scale, L0_ffn_k_scale, L0_ffn_Wo, L0_ffn_ln_g, L0_ffn_ln_b, L0_ffn_W1, L0_ffn_b1, L0_ffn_W2, L0_ffn_b2):
    import jax
    import jax.numpy as jnp

    def _L0_xattn_ref(q_in, k_in, v_in, key_padding_mask, Wq, bq, Wk, bk, Wv, bv, Wo, bo):
        import jax, jax.numpy as jnp
        import numpy as np
        DIM = 128
        N_HEAD = 16
        BS, QLEN, KLEN = (4, 256, 256)
        bs, q_len, _ = q_in.shape
        k_len = k_in.shape[1]
        h = N_HEAD
        d = DIM // h
        q = (q_in @ Wq + bq).reshape(bs, q_len, h, d).transpose(0, 2, 1, 3)
        k = (k_in @ Wk + bk).reshape(bs, k_len, h, d).transpose(0, 2, 1, 3)
        v = (v_in @ Wv + bv).reshape(bs, k_len, h, d).transpose(0, 2, 1, 3)
        score = jnp.einsum('bhqd,bhkd->bhqk', q, k) / jnp.sqrt(jnp.float32(d))
        mask = key_padding_mask[:, None, None, :]
        score = jnp.where(mask, jnp.float32(-1e+30), score)
        attn = jax.nn.softmax(score, axis=-1)
        out = jnp.einsum('bhqk,bhkd->bhqd', attn, v).transpose(0, 2, 1, 3).reshape(bs, q_len, DIM)
        return out @ Wo + bo

    def _L0_ffn_ref(x, Wqkv, q_scale, k_scale, Wo, ln_g, ln_b, W1, b1, W2, b2):
        import jax, jax.numpy as jnp
        import numpy as np
        DIM = 128
        DEPTH = 6
        HEADS = 16
        DIM_HEAD = 64
        WINDOW = 32
        INNER = HEADS * DIM_HEAD
        DIM_INNER = int(DIM * 4 * 2 / 3)
        QK_SCALE = 8.0

        def shift_tokens(t):
            a, s = jnp.split(t, 2, -1)
            s = jnp.pad(s, ((0, 0), (1, 0), (0, 0)))[:, :-1]
            return jnp.concatenate([a, s], -1)

        def l2norm(t):
            return t / jnp.maximum(jnp.linalg.norm(t, axis=-1, keepdims=True), 1e-12)

        def rotate_half(x):
            x1, x2 = jnp.split(x, 2, -1)
            return jnp.concatenate([-x2, x1], -1)

        def rotary_tables(n):
            half = jnp.arange(0, DIM_HEAD, 2, dtype=jnp.float32)
            inv_freq = 1.0 / 10000.0 ** (half / DIM_HEAD)
            t = jnp.arange(n, dtype=jnp.float32)
            freqs = t[:, None] * inv_freq[None, :]
            freqs = jnp.concatenate([freqs, freqs], -1)
            base_scale = (half + 0.4 * DIM_HEAD) / (1.4 * DIM_HEAD)
            power = (t - n // 2) / (WINDOW // 2)
            scale = base_scale[None, :] ** power[:, None]
            scale = jnp.concatenate([scale, scale], -1)
            return (freqs, scale)

        def local_attention(q, k, v):
            b, h, n, d = q.shape
            w = WINDOW
            nw = n // w
            bq = q.reshape(b, h, nw, w, d)
            bk = k.reshape(b, h, nw, w, d)
            bv = v.reshape(b, h, nw, w, d)

            def look(t):
                p = jnp.pad(t, ((0, 0), (0, 0), (1, 0), (0, 0), (0, 0)))
                return jnp.concatenate([p[:, :, :nw], p[:, :, 1:]], axis=3)
            bk2, bv2 = (look(bk), look(bv))
            seq = jnp.arange(n).reshape(nw, w)
            seq_p = jnp.pad(seq, ((1, 0), (0, 0)), constant_values=-1)
            jt = jnp.concatenate([seq_p[:nw], seq_p[1:]], axis=1)
            it = seq[:, :, None]
            jb = jt[:, None, :]
            mask = (it < jb) | (it > jb + w) | (jb == -1)
            sim = jnp.einsum('bhwie,bhwje->bhwij', bq, bk2) * QK_SCALE
            sim = jnp.where(mask, -jnp.finfo(sim.dtype).max, sim)
            attn = jax.nn.softmax(sim, -1)
            out = jnp.einsum('bhwij,bhwje->bhwie', attn, bv2)
            return out.reshape(b, h, n, d)

        def attn_layer(x, Wqkv, qs, ksc, Wo):
            b, n, _ = x.shape
            qkv = x @ Wqkv
            q, k, v = jnp.split(qkv, 3, -1)
            sh = lambda t: t.reshape(b, n, HEADS, DIM_HEAD).transpose(0, 2, 1, 3)
            q, k, v = (sh(q), sh(k), sh(v))
            q = l2norm(q) * qs
            k = l2norm(k) * ksc
            freqs, scale = rotary_tables(n)
            cos, sin = (jnp.cos(freqs), jnp.sin(freqs))
            q = q * cos * scale + rotate_half(q) * sin * scale
            inv = 1.0 / scale
            k = k * cos * inv + rotate_half(k) * sin * inv
            out = local_attention(q, k, v)
            out = out.transpose(0, 2, 1, 3).reshape(b, n, INNER)
            return out @ Wo

        def ffn_layer(x, g, bln, W1, b1, W2, b2):
            mu = x.mean(-1, keepdims=True)
            var = ((x - mu) ** 2).mean(-1, keepdims=True)
            xn = (x - mu) / jnp.sqrt(var + 1e-05) * g + bln
            hg = xn @ W1 + b1
            a, gate = jnp.split(hg, 2, -1)
            return a * jax.nn.gelu(gate, approximate=False) @ W2 + b2
        for i in range(DEPTH):
            x = attn_layer(shift_tokens(x), Wqkv[i], q_scale[i], k_scale[i], Wo[i]) + x
            x = ffn_layer(shift_tokens(x), ln_g[i], ln_b[i], W1[i], b1[i], W2[i], b2[i]) + x
        return x
    x = x + jnp.tanh(g_xattn[0]) * _L0_xattn_ref(_layernorm(x, axis=-1), ctx_1024, ctx_1024, mask_BxS2_bf0, L0_xattn_Wq, L0_xattn_bq, L0_xattn_Wk, L0_xattn_bk, L0_xattn_Wv, L0_xattn_bv, L0_xattn_Wo, L0_xattn_bo)
    x = x + jnp.tanh(g_ffn[0]) * _L0_ffn_ref(_layernorm(x, axis=-1), L0_ffn_Wqkv, L0_ffn_q_scale, L0_ffn_k_scale, L0_ffn_Wo, L0_ffn_ln_g, L0_ffn_ln_b, L0_ffn_W1, L0_ffn_b1, L0_ffn_W2, L0_ffn_b2)
    return x

_drawn_inputs = setup_inputs


def setup_inputs(seed=0):
    import zlib

    import numpy as np

    out = dict(_drawn_inputs(seed))
    spreads = {'L0_xattn_bq': (0.0, 0.418),
     'L0_xattn_bk': (0.0, 0.8),
     'L0_xattn_bv': (0.0, 0.1),
     'L0_xattn_bo': (0.0, 0.1),
     'L0_ffn_q_scale': (1.0, 0.2),
     'L0_ffn_k_scale': (1.0, 0.2),
     'L0_ffn_ln_g': (1.0, 0.6),
     'L0_ffn_ln_b': (0.0, 0.723),
     'L0_ffn_b1': (0.0, 0.1),
     'L0_ffn_b2': (0.0, 0.1)}
    factors = {}
    for name, (base, spread) in spreads.items():
        noise = np.random.default_rng([zlib.crc32(name.encode()), seed]).standard_normal(out[name].shape)
        drawn = base * np.exp(spread * noise) if base else spread * noise
        out[name] = jnp.asarray(drawn.astype(out[name].dtype))
    for name, factor in factors.items():
        out[name] = (out[name] * factor).astype(out[name].dtype)
    return out
```

```python
from contextlib import ExitStack

import concourse.bass as bass
from concourse import mybir

ALU = mybir.AluOpType
ACT = mybir.ActivationFunctionType
AX = mybir.AxisListType
F32 = mybir.dt.float32
BF16 = mybir.dt.bfloat16
U8 = mybir.dt.uint8

P = 128
BATCH, SEQ, DIM = 4, 256, 128
TILES = SEQ // P
TOKENS = BATCH * SEQ
XHEADS = 16
XDIM = DIM // XHEADS
GROUP = 32
PER = P // GROUP
MGROUPS = XHEADS // PER
DEPTH = 6
HEADS, HDIM, WIN = 16, 64, 32
INNER = HEADS * HDIM
PAIRS = HEADS // 2
QUADS = P // WIN
WINDOWS = SEQ // WIN
STEPS = DEPTH * BATCH
QK_SCALE = 8.0
FFN = DIM * 4 * 2 // 3
CHUNKS = [(0, 128), (128, 128), (256, FFN - 256)]
V_MOVES = 4 * QUADS
LCOLS = 2 * len(CHUNKS) + 3


class Signal:

    def __init__(self, sem, per=1, before=0):
        self.sem, self.per, self.before = sem, per, before

    def upto(self, n, k=None):
        return n * self.per + (self.before + (self.per if k is None else k))


def build(nc, x, ctx, mask, g_xattn, g_ffn, Wq, Wk, Wv, Wxo, bv, xcolumns,
          Wqkv, q_scale, k_scale, Wo, W1, W2, columns,
          t_cos, t_sin, t_mask, t_ident, t_spread, t_maskrow, t_one, out):
    DVE_XT, DVE_CT, DVE_C1, DVE_LN1, DVE_C2 = 9, 10, 11, 13, 14
    POOL_CONST, POOL_ALL = 4, 14
    with ExitStack() as stack:
        def sb(name, shape, dt=F32):
            return stack.enter_context(nc.sbuf_tensor(name, shape, dt))

        def sem(name):
            return stack.enter_context(nc.semaphore(name))

        ident = sb("ident", [P, P])
        ident_bf = sb("ident_bf", [P, P], BF16)
        window_mask_f = sb("window_mask_f", [P, TILES, 64])
        window_mask = sb("window_mask", [P, TILES, 8, 64], BF16)
        mean_of = sb("mean_of", [P, P])
        eps = sb("eps", [P, 1])
        spread = sb("spread", [P, P])
        maskrow_at = sb("maskrow_at", [1, P])
        one_at = sb("one_at", [P, 1])
        x_in = sb("x_in", [P, BATCH * TILES, DIM])
        mask_u8 = sb("mask_u8", [1, TOKENS], U8)
        mask_row = sb("mask_row", [1, TOKENS])
        gates = sb("gates", [P, 2])
        tgate = sb("tgate", [P, 2])

        xT = sb("xT", [P, TOKENS])
        x2T = sb("x2T", [P, TOKENS])

        wv_in = sb("wv_in", [P, DIM])
        wxo_pad = sb("wxo_pad", [P, MGROUPS, DIM])
        xcol = sb("xcol", [P, 2 * MGROUPS + 1])
        bq_pad, bk_pad, bxo = xcol[:, 0:MGROUPS], xcol[:, MGROUPS:2 * MGROUPS], xcol[:, 2 * MGROUPS:]
        bv_row = sb("bv_row", [P, DIM])
        c_bT = sb("c_bT", [P, SEQ])
        xmax = sb("xmax", [P, 4, TILES])
        xneg = sb("xneg", [P, 4, TILES])
        xo = sb("xo", [P, SEQ])
        xrec = sb("xrec", [P, SEQ])
        xtmp = sb("xtmp", [P, SEQ])

        w_qkv = sb("w_qkv", [P, 3 * INNER])
        w_o = sb("w_o", [P, PAIRS, DIM])
        w_1 = sb("w_1", [P, 2 * FFN])
        w_2 = sb("w_2", [P, len(CHUNKS), DIM])
        lcol = sb("lcol", [P, LCOLS])
        b_1 = lcol[:, 0:6].rearrange("p (h c) -> p h c", h=2)
        ln_gb, b_2 = lcol[:, 6:8], lcol[:, 8:9]
        cos_in = sb("cos_in", [P, TILES, 2 * HDIM])
        sin_in = sb("sin_in", [P, TILES, 2 * HDIM])
        scales = sb("scales", [P, DEPTH, 2 * HDIM])
        rot_cos = sb("rot_cos", [P, DEPTH * TILES, 2 * HDIM])
        rot_sin = sb("rot_sin", [P, DEPTH * TILES, 2 * HDIM])

        xs = sb("xs", [P, SEQ])
        raw = sb("raw", [P, TILES, 2 * INNER])
        squares = sb("squares", [P, 2 * INNER])
        by_cos = sb("by_cos", [P, 2 * INNER])
        by_sin = sb("by_sin", [P, 2 * INNER])
        norm2 = sb("norm2", [P, TILES, 2 * HEADS])
        norm = sb("norm", [P, TILES, 2 * HEADS])
        norm_c = sb("norm_c", [P, TILES, 2 * HEADS])
        inv_norm = sb("inv_norm", [P, TILES, 2 * HEADS])
        v_tok = sb("v_tok", [P, TILES, INNER])
        v_win = sb("v_win", [P, WINDOWS, INNER // 2])
        qkT = sb("qkT", [P, 2 * PAIRS, SEQ])

        row_max = sb("row_max", [P, TILES, HEADS])
        row_sum = sb("row_sum", [P, TILES, HEADS])
        row_inv = sb("row_inv", [P, TILES, HEADS])
        probs = sb("probs", [P, TILES, HEADS * 64])
        probsT = sb("probsT", [P, TILES, PAIRS * P])
        att = sb("att", [P, TILES, INNER])
        attT = sb("attT", [P, PAIRS, SEQ])
        x1T = sb("x1T", [P, SEQ])
        xfT = sb("xfT", [P, SEQ])
        ln_big = by_sin
        centred = sb("centred", [P, SEQ])
        centred2 = sb("centred2", [P, SEQ])
        std = sb("std", [P, SEQ])
        rstd = sb("rstd", [P, SEQ])
        normed = sb("normed", [P, SEQ])
        ffn_in = sb("ffn_in", [P, SEQ])
        gelu = sb("gelu", [P, len(CHUNKS), SEQ])
        hidden = sb("hidden", [P, len(CHUNKS), SEQ])

        c_in = att[:, 0, :].rearrange("p (a d) -> p a d", d=DIM)
        xon = att[:, 1, :].rearrange("p (m s) -> p m s", m=MGROUPS)
        wq_pad = attT[:, 0:2, :].rearrange("p a s -> p (a s)").rearrange("p (h g) -> p h g", g=GROUP)
        wk_pad = attT[:, 2:4, :].rearrange("p a s -> p (a s)").rearrange("p (h g) -> p h g", g=GROUP)
        v_aug = attT[:, 4:8, :].rearrange("p a s -> p (a s)").rearrange("p (t h g) -> p t h g", t=TILES, g=GROUP)
        xn_big = by_cos[:, 0:TOKENS]
        sq_big = by_cos[:, TOKENS:2 * TOKENS]
        sd_big = ln_big[:, 0:TOKENS]
        rs_big = ln_big[:, TOKENS:2 * TOKENS]
        cT = squares[:, 0:TOKENS]
        xnT = squares[:, TOKENS:2 * TOKENS]
        qT_x = raw[:, 0, 0:MGROUPS * SEQ].rearrange("p (m s) -> p m s", m=MGROUPS)
        kT_x = raw[:, 0, MGROUPS * SEQ:2 * MGROUPS * SEQ].rearrange("p (m s) -> p m s", m=MGROUPS)
        p_x = raw[:, 1, :].rearrange("p (r q k) -> p r q k", r=4, q=TILES)
        pT_x = v_tok[:, 0, :].rearrange("p (r k q) -> p r k q", r=2, k=TILES)

        pe_lo = [stack.enter_context(nc.psum_tensor(f"ps_s{i}", [P, 1024], F32)) for i in range(2)]
        pe_hi = [stack.enter_context(nc.psum_tensor(f"ps_g{i}", [P, 1024], F32)) for i in range(2)]

        def bank(i):
            t = (pe_lo + pe_hi)[i // 2]
            return t[:, 512 * (i % 2):512 * (i % 2) + 512]

        loaded = sem("loaded")
        pre_dve = sem("pre_dve")
        pre_pool = sem("pre_pool")
        pre_act = sem("pre_act")
        pre_pe = sem("pre_pe")
        c_copied = Signal(sem("c_copied"))
        xq_mm = Signal(sem("xq_mm"))
        xk_mm = Signal(sem("xk_mm"))
        xv_mm = Signal(sem("xv_mm"))
        xq_out = Signal(sem("xq_out"), MGROUPS)
        xk_out = Signal(sem("xk_out"), MGROUPS)
        xv_out = Signal(sem("xv_out"), 1)
        xs_mm = Signal(sem("xs_mm"), XHEADS)
        x_max = Signal(sem("x_max"), XHEADS)
        x_neg = Signal(sem("x_neg"), XHEADS)
        x_exp = Signal(sem("x_exp"), 2 * XHEADS)
        xt_mm = Signal(sem("xt_mm"), XHEADS)
        xt_out = Signal(sem("xt_out"), XHEADS)
        xo_mm = Signal(sem("xo_mm"), XHEADS)
        xo_out = Signal(sem("xo_out"), MGROUPS)
        xsum_mm = Signal(sem("xsum_mm"), MGROUPS)
        xrec_done = Signal(sem("xrec_done"), MGROUPS)
        xon_done = Signal(sem("xon_done"), MGROUPS)
        xy_mm = Signal(sem("xy_mm"))
        xy_scaled = Signal(sem("xy_scaled"))
        xy_done = Signal(sem("xy_done"))
        qkv_loaded = sem("qkv_loaded")
        small_loaded = sem("small_loaded")
        x_ready = Signal(sem("x_ready"), 1, 1)
        xs_ready = Signal(sem("xs_ready"), 2)
        qkv_mm = Signal(sem("qkv_mm"), 6)
        qkv_copied = Signal(sem("qkv_copied"), 6)
        squared = Signal(sem("squared"), 4)
        norm2_done = Signal(sem("norm2_done"), 2)
        norm_done = Signal(sem("norm_done"), 2)
        normc_done = Signal(sem("normc_done"), 2)
        inv_done = Signal(sem("inv_done"), 2)
        cos_done = Signal(sem("cos_done"), 2)
        sin_done = Signal(sem("sin_done"), 4)
        rot_done = Signal(sem("rot_done"), 2)
        qk_done = Signal(sem("qk_done"), 2)
        qkT_mm = Signal(sem("qkT_mm"), 4)
        qkT_out = Signal(sem("qkT_out"), 4)
        v_moved = Signal(sem("v_moved"), 16 * V_MOVES)
        s_mm = Signal(sem("s_mm"), 2)
        max_done = Signal(sem("max_done"), 2)
        shifted = Signal(sem("shifted"), 2)
        exp_done = Signal(sem("exp_done"), 2)
        sum_done = Signal(sem("sum_done"), 2)
        rinv_done = Signal(sem("rinv_done"), 2)
        pT_mm = Signal(sem("pT_mm"), 2)
        pT_out = Signal(sem("pT_out"), 2)
        pv_mm = Signal(sem("pv_mm"), 2)
        att_done = Signal(sem("att_done"), 2)
        attT_mm = Signal(sem("attT_mm"), 2)
        attT_out = Signal(sem("attT_out"), 2)
        y_mm = Signal(sem("y_mm"))
        x1_done = Signal(sem("x1_done"), 3)
        mean_mm = Signal(sem("mean_mm"))
        centre_done = Signal(sem("centre_done"))
        csq_done = Signal(sem("csq_done"))
        var_mm = Signal(sem("var_mm"))
        std_done = Signal(sem("std_done"))
        rstd_done = Signal(sem("rstd_done"))
        normed_done = Signal(sem("normed_done"))
        ffnin_done = Signal(sem("ffnin_done"))
        gate_mm = Signal(sem("gate_mm"), 2)
        up_mm = Signal(sem("up_mm"))
        gelu_done = Signal(sem("gelu_done"), 3)
        hid_done = Signal(sem("hid_done"), 3)
        down_mm = Signal(sem("down_mm"))
        fin_done = sem("fin_done")
        fin_mm = sem("fin_mm")
        fin_copied = sem("fin_copied")
        stored = sem("stored")

        def token_tiles(a):
            return a.rearrange("b (t p) d -> p (b t) d", p=P)

        LOADS = []

        def wait(engine, signal, n, k=None):
            engine.wait_ge(signal.sem, signal.upto(n, k))

        block = stack.enter_context(nc.Block())

        @block.sync
        def _(sp):
            def load(dst, src):
                LOADS.append(1)
                sp.dma_start(dst, src).then_inc(loaded, 16)

            load(ident[:], t_ident)
            load(x_in[:], token_tiles(x))
            load(c_in, token_tiles(ctx))
            load(wq_pad, Wq)
            load(wk_pad, Wk)
            load(wxo_pad[:], Wxo)
            load(xcol[:], xcolumns)
            load(wv_in[:], Wv)
            load(mask_u8[:], mask.rearrange("(o b) s -> o (b s)", o=1))
            load(gates[:, 0:1], g_xattn.rearrange("(o d) -> o d", o=1).partition_broadcast(P))
            load(gates[:, 1:2], g_ffn.rearrange("(o d) -> o d", o=1).partition_broadcast(P))
            load(bv_row[:], bv.rearrange("(o d) -> o d", o=1).partition_broadcast(P))
            load(spread[:], t_spread)
            load(maskrow_at[:], t_maskrow)
            load(one_at[:], t_one)
            load(cos_in[:], t_cos.rearrange("(t p) d -> p t d", p=P))
            load(sin_in[:], t_sin.rearrange("(t p) d -> p t d", p=P))
            load(window_mask_f[:], t_mask.rearrange("(t p) d -> p t d", p=P))
            load(scales[:, :, 0:HDIM], q_scale.rearrange("(o l) d -> o l d", o=1).partition_broadcast(P))
            load(scales[:, :, HDIM:], k_scale.rearrange("(o l) d -> o l d", o=1).partition_broadcast(P))
            def load_qkv(layer):
                sp.dma_start(w_qkv[:], Wqkv[layer]).then_inc(qkv_loaded, 16)

            def load_small(layer):
                sp.dma_start(w_o[:], Wo[layer].rearrange("(c p) d -> p c d", p=P)).then_inc(small_loaded, 16)
                sp.dma_start(w_1[:], W1[layer]).then_inc(small_loaded, 16)
                sp.dma_start(w_2[:], W2[layer].rearrange("(c p) d -> p c d", p=P)).then_inc(small_loaded, 16)
                sp.dma_start(lcol[:], columns[layer]).then_inc(small_loaded, 16)

            def move_values(n, first=False):
                wait(sp, qkv_copied, n)
                if not first:
                    wait(sp, pv_mm, n - 1)
                for odd in range(2):
                    cols = slice(512 * odd, 512 * odd + 512)
                    for c in range(QUADS):
                        src = v_tok[WIN * c:WIN * c + WIN, :, cols]
                        own = slice(64 * odd + 32, 64 * odd + 64)
                        before = slice(64 * odd, 64 * odd + 32)
                        sp.dma_start(v_win[own, c:WINDOWS:QUADS, :], src).then_inc(v_moved.sem, 16)
                        if c < QUADS - 1:
                            sp.dma_start(v_win[before, c + 1:WINDOWS:QUADS, :], src).then_inc(v_moved.sem, 16)
                        else:
                            sp.dma_start(v_win[before, QUADS, :], src[:, 0]).then_inc(v_moved.sem, 16)

            load_qkv(0)
            load_small(0)
            move_values(0, first=True)
            with sp.Fori(1, DEPTH) as layer:
                with sp.Fori(0, BATCH - 1) as j:
                    move_values(layer * BATCH + j - (BATCH - 1))
                wait(sp, qkv_mm, layer * BATCH - 1)
                load_qkv(layer)
                move_values(layer * BATCH)
                wait(sp, x_ready, layer * BATCH - 1)
                load_small(layer)
            with sp.Fori(STEPS - BATCH + 1, STEPS) as n:
                move_values(n)

            sp.wait_ge(fin_copied, 1)
            sp.dma_start(token_tiles(out), x_in[:]).then_inc(stored, 16)
            sp.wait_ge(stored, 16)

        n_loads = len(LOADS)
        SMALLS = 4

        @block.gpsimd
        def _(pool):
            nc.gpsimd.memset(v_aug, 0.0).then_inc(pre_pool, 1)
            pool.wait_ge(pre_pool, 1)
            nc.gpsimd.memset(v_aug[:, :, :, XDIM:XDIM + 1], 1.0).then_inc(pre_pool, 1)
            nc.gpsimd.memset(mean_of[:], 1.0 / DIM).then_inc(pre_pool, 1)
            nc.gpsimd.memset(eps[:], 1e-5).then_inc(pre_pool, 1)
            pool.wait_ge(loaded, 16 * n_loads)
            for t in range(TILES):
                nc.gpsimd.tensor_tensor(rot_cos[:, t::TILES, :], cos_in[:, t:t + 1, :].to_broadcast([P, DEPTH, 2 * HDIM]),
                                        scales[:], ALU.mult).then_inc(pre_pool, 1)
                for qk in range(2):
                    for half in range(2):
                        d = HDIM * qk + 32 * half
                        o = HDIM * qk + 32 * (1 - half)
                        nc.gpsimd.tensor_tensor(rot_sin[:, t::TILES, d:d + 32],
                                                sin_in[:, t:t + 1, d:d + 32].to_broadcast([P, DEPTH, 32]),
                                                scales[:, :, o:o + 32], ALU.mult).then_inc(pre_pool, 1)

            pool.wait_ge(pre_dve, DVE_CT)
            nc.gpsimd.tensor_copy(c_bT[:], cT[:, 0:SEQ]).then_inc(c_copied.sem, 1)
            with pool.Fori(1, BATCH) as b:
                wait(pool, xv_mm, b - 1)
                nc.gpsimd.tensor_copy(c_bT[:], cT[:, bass.ds(b * SEQ, SEQ)]).then_inc(c_copied.sem, 1)

            def prepare(n, first=False):
                wait(pool, x_ready, 0 if first else n - 1, 0)
                if not first:
                    wait(pool, qkv_mm, n - 1)
                    wait(pool, cos_done, n - 1)
                b = n % BATCH
                nc.gpsimd.tensor_copy(xs[0:64, :], xT[0:64, bass.ds(b * SEQ, SEQ)]).then_inc(xs_ready.sem, 1)
                wait(pool, xs_ready, n, 1)
                nc.gpsimd.tensor_copy(xs[64:P, 1:SEQ], xT[64:P, bass.ds(b * SEQ, SEQ - 1)]).then_inc(xs_ready.sem, 1)
                wait(pool, xs_ready, n)
                layer = n // BATCH
                for t in range(TILES):
                    wait(pool, qkv_copied, n, 3 * t + 2)
                    if t:
                        wait(pool, rot_done, n, 1)
                    elif not first:
                        wait(pool, rot_done, n - 1)
                    nc.gpsimd.tensor_tensor(
                        by_cos[:].rearrange("p (k h d) -> p k h d", k=2, d=HDIM),
                        raw[:, t, :].rearrange("p (k h d) -> p k h d", k=2, d=HDIM),
                        rot_cos[:, bass.ds(layer * TILES + t, 1), :].rearrange("p o (k h d) -> p (o k) h d", k=2, h=1)
                        .to_broadcast([P, 2, HEADS, HDIM]), ALU.mult).then_inc(cos_done.sem, 1)

            prepare(0, first=True)
            with pool.Fori(0, STEPS - 1) as n:
                prepare(n + 1)

        @block.tensor
        def _(pe):
            pe.wait_ge(loaded, 16 * n_loads)
            for i in range(BATCH * TILES):
                mm = nc.tensor.transpose(pe_lo[0][:, P * i:P * i + P], x_in[:, i, :], ident[:])
            mm.then_inc(pre_pe, 1)
            for i in range(BATCH * TILES):
                mm = nc.tensor.transpose(pe_lo[1][:, P * i:P * i + P], c_in[:, i, :], ident[:])
            mm.then_inc(pre_pe, 1)

            def big_mean(src, out_ps):
                for j in range(2):
                    mm = nc.tensor.matmul(out_ps[:, 512 * j:512 * j + 512], mean_of[:], src[:, 512 * j:512 * j + 512],
                                          start=True, stop=True)
                mm.then_inc(pre_pe, 1)

            pe.wait_ge(pre_dve, DVE_XT)
            pe.wait_ge(pre_pool, POOL_CONST)
            big_mean(xT, pe_hi[0])
            pe.wait_ge(pre_act, 2)
            big_mean(sq_big, pe_hi[1])

            pe.wait_ge(pre_dve, DVE_LN1)
            with pe.Fori(0, BATCH) as b:
                bs = bass.ds(b * SEQ, SEQ)
                for m in range(MGROUPS):
                    mm = nc.tensor.matmul(pe_lo[0][:, SEQ * m:SEQ * m + SEQ], wq_pad[:, PER * m:PER * m + PER, :],
                                          xnT[:, bs], start=True, stop=True)
                mm.then_inc(xq_mm.sem, 1)
                for m in range(MGROUPS):
                    o = pe_lo[1][:, SEQ * m:SEQ * m + SEQ]
                    nc.tensor.matmul(o, wk_pad[:, PER * m:PER * m + PER, :], cT[:, bs], start=True, stop=False)
                    mm = nc.tensor.matmul(o, maskrow_at[:], mask_row[0:1, bs], start=False, stop=True)
                mm.then_inc(xk_mm.sem, 1)
                wait(pe, c_copied, b)
                for t in range(TILES):
                    mm = nc.tensor.matmul(bank(4)[:, P * t:P * t + P], c_bT[:, P * t:P * t + P], wv_in[:],
                                          start=True, stop=True)
                mm.then_inc(xv_mm.sem, 1)
                wait(pe, xq_out, b)
                wait(pe, xk_out, b)
                wait(pe, xv_out, b)

                def scores(h):
                    m, g = divmod(h, PER)
                    rows = slice(GROUP * g, GROUP * g + GROUP)
                    if h >= 4:
                        wait(pe, x_exp, b, 2 * (h - 3))
                    for t in range(TILES):
                        mm = nc.tensor.matmul(bank(h % 4)[:, SEQ * t:SEQ * t + SEQ], qT_x[rows, m, P * t:P * t + P],
                                              kT_x[rows, m, :], start=True, stop=True)
                    mm.then_inc(xs_mm.sem, 1)

                def turn(h):
                    wait(pe, x_exp, b, 2 * (h + 1))
                    if h >= 2:
                        wait(pe, xt_out, b, h - 1)
                    for k in range(TILES):
                        for t in range(TILES):
                            mm = nc.tensor.transpose(bank(4 + h % 2)[:, SEQ * k + P * t:SEQ * k + P * t + P],
                                                     p_x[:, h % 4, t, P * k:P * k + P], ident[:])
                    mm.then_inc(xt_mm.sem, 1)

                def values(h):
                    m, g = divmod(h, PER)
                    wait(pe, xt_out, b, h + 1)
                    if g == 0 and m >= 2:
                        wait(pe, xrec_done, b, m - 1)
                    for k in range(TILES):
                        mm = nc.tensor.matmul(bank(6 + m % 2)[GROUP * g:GROUP * g + GROUP, 0:SEQ], v_aug[:, k, h, :],
                                              pT_x[:, h % 2, k, :], start=(k == 0), stop=(k == 1),
                                              tile_position=(0, GROUP * g))
                    mm.then_inc(xo_mm.sem, 1)

                def sums(m):
                    wait(pe, xo_out, b, m + 1)
                    nc.tensor.matmul(bank(6 + m % 2)[:, SEQ:2 * SEQ], spread[:], xo[:], start=True, stop=True)\
                        .then_inc(xsum_mm.sem, 1)

                for h in range(XHEADS + 3):
                    if h < XHEADS:
                        scores(h)
                    if 1 <= h <= XHEADS:
                        turn(h - 1)
                    if 2 <= h <= XHEADS + 1:
                        values(h - 2)
                    if h >= 6 and (h - 6) % PER == 0:
                        sums((h - 6) // PER)
                wait(pe, xon_done, b)
                for m in range(MGROUPS):
                    mm = nc.tensor.matmul(bank(4)[:, 0:SEQ], wxo_pad[:, m, :], xon[:, m, :], start=(m == 0),
                                          stop=(m == MGROUPS - 1))
                mm.then_inc(xy_mm.sem, 1)
                wait(pe, xy_scaled, b)

            pe.wait_ge(xy_done.sem, BATCH)
            big_mean(x2T, pe_hi[0])
            pe.wait_ge(pre_act, 4)
            big_mean(sq_big, pe_hi[1])
            pe.wait_ge(x_ready.sem, 1)

            def project(n, tiles):
                for t in tiles:
                    for part in range(3):
                        i = 3 * t + part
                        if i >= 2:
                            wait(pe, qkv_copied, n, i - 1)
                            if i - 2 != 2:
                                wait(pe, squared, n, {0: 1, 1: 2, 3: 3}[i - 2])
                        for j in range(2):
                            if part < 2:
                                cols = w_qkv[:, INNER * part + 512 * j:INNER * part + 512 * j + 512]
                            else:
                                cols = w_qkv[:, 2 * INNER:].rearrange("p (h o d) -> p o h d", o=2, d=HDIM)[:, j]
                            mm = nc.tensor.matmul(pe_hi[i % 2][:, 512 * j:512 * j + 512], xs[:, P * t:P * t + P], cols,
                                                  start=True, stop=True)
                        mm.then_inc(qkv_mm.sem, 1)

            def turn_qk(n, j):
                if j >= 2:
                    wait(pe, qkT_out, n, j - 1)
                for p in range(4):
                    for t in range(TILES):
                        if p == 0 and j == 0:
                            wait(pe, qk_done, n, t + 1)
                        mm = nc.tensor.transpose(pe_lo[j % 2][:, SEQ * p + P * t:SEQ * p + P * t + P],
                                                 raw[:, t, P * (4 * j + p):P * (4 * j + p) + P], ident[:])
                mm.then_inc(qkT_mm.sem, 1)

            def scores_of(n):
                wait(pe, qkT_out, n)
                for t in range(TILES):
                    ps = pe_lo[t]
                    for odd in range(2):
                        nc.tensor.matmul(ps[:, 512 * odd:512 * odd + 512], ident_bf[:], window_mask[:, t], start=True,
                                         stop=False, skip_group_check=True)
                    for h in range(HEADS):
                        rows = slice(64 * (h % 2), 64 * (h % 2) + 64)
                        for c in range(QUADS):
                            w = QUADS * t + c
                            k0 = WIN * max(w - 1, 0)
                            keys = WIN * (w + 1) - k0
                            o = 512 * (h % 2) + 64 * (h // 2) + 64 - keys
                            mm = nc.tensor.matmul(ps[WIN * c:WIN * c + WIN, o:o + keys],
                                                  qkT[rows, h // 2, WIN * w:WIN * w + WIN],
                                                  qkT[rows, PAIRS + h // 2, k0:k0 + keys],
                                                  start=False, stop=True, skip_group_check=True,
                                                  tile_position=(64 * (h % 2), WIN * c))
                    mm.then_inc(s_mm.sem, 1)

            def turn_probs(n, t):
                wait(pe, exp_done, n, t + 1)
                for p in range(PAIRS):
                    mm = nc.tensor.transpose(pe_lo[t][:, P * p:P * p + P], probs[:, t, P * p:P * p + P], ident[:])
                mm.then_inc(pT_mm.sem, 1)

            def weigh_values(n, t):
                wait(pe, pT_out, n, t + 1)
                wait(pe, v_moved, n)
                nc.tensor.matmul(pe_hi[t][:, 0:2], ident_bf[:], ident_bf[:, 0:2], start=True, stop=True)
                for h in range(HEADS):
                    odd = h % 2
                    for c in range(QUADS):
                        w = QUADS * t + c
                        r0 = 64 * odd + (32 if w == 0 else 0)
                        rows = slice(r0, 64 * odd + 64)
                        o = 512 * odd + 64 * (h // 2)
                        mm = nc.tensor.matmul(pe_hi[t][WIN * c:WIN * c + WIN, o:o + 64],
                                              probsT[rows, t, P * (h // 2) + WIN * c:P * (h // 2) + WIN * c + WIN],
                                              v_win[rows, w, 64 * (h // 2):64 * (h // 2) + 64],
                                              start=True, stop=True, skip_group_check=True,
                                              tile_position=(r0, WIN * c))
                mm.then_inc(pv_mm.sem, 1)

            def turn_att(n):
                wait(pe, att_done, n)
                for half in range(2):
                    for p in range(4):
                        for t in range(TILES):
                            mm = nc.tensor.transpose(pe_hi[half][:, SEQ * p + P * t:SEQ * p + P * t + P],
                                                     att[:, t, P * (4 * half + p):P * (4 * half + p) + P], ident[:])
                    mm.then_inc(attT_mm.sem, 1)

            def small_weights(n):
                pe.wait_ge(small_loaded, (n // BATCH + 1) * (16 * SMALLS))

            def attend_end(n, between):
                turn_att(n)
                between(0)
                wait(pe, attT_out, n)
                small_weights(n)
                for p in range(PAIRS):
                    mm = nc.tensor.matmul(bank(4)[:, 0:SEQ], w_o[:, p, :], attT[:, p, :], start=(p == 0),
                                          stop=(p == PAIRS - 1))
                mm.then_inc(y_mm.sem, 1)
                between(1)
                wait(pe, x1_done, n)
                nc.tensor.matmul(bank(5)[:, 0:SEQ], mean_of[:], xfT[:], start=True, stop=True).then_inc(mean_mm.sem, 1)
                between(2)
                wait(pe, csq_done, n)
                nc.tensor.matmul(bank(6)[:, 0:SEQ], mean_of[:], centred2[:], start=True, stop=True).then_inc(var_mm.sem, 1)
                between(3)
                wait(pe, ffnin_done, n)
                for j, (f0, fs) in enumerate(CHUNKS):
                    o = bank(7)[0:fs, SEQ * j:SEQ * j + SEQ] if j < 2 else bank(4)[0:fs, 0:SEQ]
                    mm = nc.tensor.matmul(o, w_1[:, FFN + f0:FFN + f0 + fs], ffn_in[:], start=True, stop=True)
                    if j:
                        mm.then_inc(gate_mm.sem, 1)
                for j, (f0, fs) in enumerate(CHUNKS):
                    o = bank(5)[0:fs, SEQ * j:SEQ * j + SEQ] if j < 2 else bank(6)[0:fs, 0:SEQ]
                    mm = nc.tensor.matmul(o, w_1[:, f0:f0 + fs], ffn_in[:], start=True, stop=True)
                mm.then_inc(up_mm.sem, 1)
                wait(pe, gelu_done, n)
                for j, (f0, fs) in enumerate(CHUNKS):
                    wait(pe, hid_done, n, j + 1)
                    mm = nc.tensor.matmul(bank(7)[:, 0:SEQ], w_2[0:fs, j, :], hidden[0:fs, j, :], start=(j == 0),
                                          stop=(j == 2))
                mm.then_inc(down_mm.sem, 1)

            def start_project(n):
                wait(pe, xs_ready, n)
                pe.wait_ge(qkv_loaded, (n // BATCH + 1) * 16)

            start_project(0)
            project(0, range(TILES))
            for j in range(4):
                turn_qk(0, j)
            with pe.Fori(0, STEPS - 1) as n:
                scores_of(n)
                start_project(n + 1)
                wait(pe, x_ready, n, 0)
                project(n + 1, range(TILES))
                for t in range(TILES):
                    turn_probs(n, t)
                wait(pe, qkv_copied, n + 1)
                for t in range(TILES):
                    weigh_values(n, t)
                attend_end(n, lambda j: turn_qk(n + 1, j))
            scores_of(STEPS - 1)
            wait(pe, x_ready, STEPS - 1, 0)
            for t in range(TILES):
                turn_probs(STEPS - 1, t)
                weigh_values(STEPS - 1, t)
            attend_end(STEPS - 1, lambda j: None)

            pe.wait_ge(fin_done, 1)
            for i in range(BATCH * TILES):
                mm = nc.tensor.transpose(pe_lo[0][:, P * i:P * i + P], x2T[:, P * i:P * i + P], ident[:])
            mm.then_inc(fin_mm, 1)

        @block.scalar
        def _(act):
            act.wait_ge(loaded, 16 * n_loads)
            nc.scalar.activation(tgate[:], gates[:], ACT.Tanh).then_inc(pre_act, 1)

            def norm_part(k):
                act.wait_ge(pre_dve, k)
                nc.scalar.activation(sq_big, xn_big, ACT.Square).then_inc(pre_act, 1)

            norm_part(DVE_C1)
            act.wait_ge(pre_pe, 4)
            act.wait_ge(pre_pool, POOL_CONST)
            nc.scalar.activation(sd_big, pe_hi[1][:], ACT.Sqrt, bias=eps[:, 0:1]).then_inc(pre_act, 1)

            with act.Fori(0, BATCH) as b:
                wait(act, xq_mm, b)
                for m in range(MGROUPS):
                    nc.scalar.activation(qT_x[:, m, :], pe_lo[0][:, SEQ * m:SEQ * m + SEQ], ACT.Identity,
                                         bias=bq_pad[:, m:m + 1]).then_inc(xq_out.sem, 1)
                wait(act, xk_mm, b)
                for m in range(MGROUPS):
                    nc.scalar.activation(kT_x[:, m, :], pe_lo[1][:, SEQ * m:SEQ * m + SEQ], ACT.Identity,
                                         bias=bk_pad[:, m:m + 1]).then_inc(xk_out.sem, 1)

                def copy_turned(h):
                    wait(act, xt_mm, b, h + 1)
                    if h >= 2:
                        wait(act, xo_mm, b, h - 1)
                    nc.scalar.copy(pT_x[:, h % 2], bank(4 + h % 2).rearrange("p (k q) -> p k q", k=TILES))\
                        .then_inc(xt_out.sem, 1)

                for h in range(XHEADS + 1):
                    if h < XHEADS:
                        wait(act, x_neg, b, h + 1)
                        if h >= 4:
                            wait(act, xt_mm, b, h - 3)
                        for t in range(TILES):
                            nc.scalar.activation(p_x[:, h % 4, t, :], bank(h % 4)[:, SEQ * t:SEQ * t + SEQ], ACT.Exp,
                                                 bias=xneg[:, h % 4, t:t + 1], scale=float(XDIM) ** -0.5)\
                                .then_inc(x_exp.sem, 1)
                    if h:
                        copy_turned(h - 1)

            norm_part(DVE_C2)
            act.wait_ge(pre_pe, 6)
            nc.scalar.activation(sd_big, pe_hi[1][:], ACT.Sqrt, bias=eps[:, 0:1]).then_inc(pre_act, 1)

            def take_qk(n, t, part, first):
                i = 3 * t + part
                wait(act, qkv_mm, n, i + 1)
                if not first:
                    wait(act, qkT_mm, n - 1)
                cols = slice(INNER * part, INNER * part + INNER)
                nc.scalar.copy(raw[:, t, cols], pe_hi[i % 2][:]).then_inc(qkv_copied.sem, 1)
                if t:
                    wait(act, norm2_done, n, 1)
                elif not first:
                    wait(act, norm2_done, n - 1)
                nc.scalar.activation(squares[:, cols], pe_hi[i % 2][:], ACT.Square).then_inc(squared.sem, 1)

            def take_v(n, t, first):
                i = 3 * t + 2
                wait(act, qkv_mm, n, i + 1)
                if not first:
                    wait(act, v_moved, n - 1)
                nc.scalar.copy(v_tok[:, t, :], pe_hi[i % 2][:]).then_inc(qkv_copied.sem, 1)

            def root(n, t):
                wait(act, norm2_done, n, t + 1)
                nc.scalar.activation(norm[:, t, :], norm2[:, t, :], ACT.Sqrt).then_inc(norm_done.sem, 1)

            def copy_qkT(n, j):
                wait(act, qkT_mm, n, j + 1)
                nc.scalar.copy(qkT[:, 4 * j:4 * j + 4, :],
                               pe_lo[j % 2][:].rearrange("p (a s) -> p a s", a=4)).then_inc(qkT_out.sem, 1)

            def exponent(n, t):
                wait(act, shifted, n, t + 1)
                nc.scalar.activation(probs[:, t, :], probs[:, t, :], ACT.Exp, scale=QK_SCALE).then_inc(exp_done.sem, 1)

            def copy_probsT(n, t):
                wait(act, pT_mm, n, t + 1)
                nc.scalar.copy(probsT[:, t, :], pe_lo[t][:]).then_inc(pT_out.sem, 1)

            def copy_attT(n):
                for half in range(2):
                    wait(act, attT_mm, n, half + 1)
                    nc.scalar.copy(attT[:, 4 * half:4 * half + 4, :],
                                   pe_hi[half][:].rearrange("p (a s) -> p a s", a=4)).then_inc(attT_out.sem, 1)

            def attend_end(n, between):
                copy_attT(n)
                between(0)
                between(1)
                wait(act, centre_done, n)
                nc.scalar.activation(centred2[:], centred[:], ACT.Square).then_inc(csq_done.sem, 1)
                between(2)
                wait(act, var_mm, n)
                nc.scalar.activation(std[:], bank(6)[:, 0:SEQ], ACT.Sqrt, bias=eps[:, 0:1]).then_inc(std_done.sem, 1)
                between(3)
                for j, (f0, fs) in enumerate(CHUNKS):
                    wait(act, gate_mm, n, max(j, 1))
                    src = bank(7)[0:fs, SEQ * j:SEQ * j + SEQ] if j < 2 else bank(4)[0:fs, 0:SEQ]
                    nc.scalar.activation(gelu[0:fs, j, :], src, ACT.Gelu, bias=b_1[0:fs, 1, j:j + 1])\
                        .then_inc(gelu_done.sem, 1)

            def prepare(n, first=False):
                for t in range(TILES):
                    take_qk(n, t, 0, first)
                    take_qk(n, t, 1, first)
                    take_v(n, t, first)

            prepare(0, first=True)
            for t in range(TILES):
                root(0, t)
            for j in range(4):
                copy_qkT(0, j)
            with act.Fori(0, STEPS - 1) as n:
                exponent(n, 0)
                take_qk(n + 1, 0, 0, False)
                exponent(n, 1)
                take_qk(n + 1, 0, 1, False)
                take_v(n + 1, 0, False)
                root(n + 1, 0)
                take_qk(n + 1, 1, 0, False)
                take_qk(n + 1, 1, 1, False)
                take_v(n + 1, 1, False)
                copy_probsT(n, 0)
                copy_probsT(n, 1)
                root(n + 1, 1)
                attend_end(n, lambda j: copy_qkT(n + 1, j))
            exponent(STEPS - 1, 0)
            exponent(STEPS - 1, 1)
            copy_probsT(STEPS - 1, 0)
            copy_probsT(STEPS - 1, 1)
            attend_end(STEPS - 1, lambda j: None)

            act.wait_ge(fin_mm, 1)
            nc.scalar.copy(x_in[:], pe_lo[0][:].rearrange("p (a d) -> p a d", a=BATCH * TILES)).then_inc(fin_copied, 1)

        @block.vector
        def _(dve):
            done = [0]

            def link(ins):
                done[0] += 1
                ins.then_inc(pre_dve, 1)
                dve.wait_ge(pre_dve, done[0])

            dve.wait_ge(loaded, 16 * n_loads)
            link(nc.vector.tensor_copy(ident_bf[:], ident[:]))
            link(nc.vector.memset(xs[64:P, 0:1], 0.0))
            link(nc.vector.memset(xfT[64:P, 0:1], 0.0))
            for t in range(TILES):
                link(nc.vector.tensor_copy(window_mask[:, t], window_mask_f[:, t:t + 1, :].to_broadcast([P, 8, 64])))
            link(nc.vector.tensor_copy(mask_row[:], mask_u8[:]))
            link(nc.vector.tensor_scalar(mask_row[:], mask_row[:], -1e30 * float(XDIM) ** 0.5, None, ALU.mult))
            link(nc.vector.tensor_tensor(bq_pad, bq_pad, one_at[:].to_broadcast([P, MGROUPS]), ALU.add))
            dve.wait_ge(pre_pe, 1)
            link(nc.vector.tensor_copy(xT[:], pe_lo[0][:]))
            assert done[0] == DVE_XT
            dve.wait_ge(pre_pe, 2)
            link(nc.vector.tensor_copy(cT, pe_lo[1][:]))
            assert done[0] == DVE_CT

            def big_norm(src, dst, k, marks):
                dve.wait_ge(pre_pe, k)
                link(nc.vector.tensor_tensor(xn_big, src, pe_hi[0][:], ALU.subtract))
                assert done[0] == marks[0]
                dve.wait_ge(pre_act, marks[1])
                link(nc.vector.reciprocal(rs_big, sd_big))
                ins = nc.vector.tensor_tensor(dst, xn_big, rs_big, ALU.mult)
                return ins

            link(big_norm(xT[:], xnT, 3, (DVE_C1, 3)))
            assert done[0] == DVE_LN1

            with dve.Fori(0, BATCH) as b:
                bs = bass.ds(b * SEQ, SEQ)
                wait(dve, xv_mm, b)
                nc.vector.tensor_tensor(
                    v_aug[:, :, :, 0:XDIM], bank(4)[:, 0:TILES * P].rearrange("p (t h d) -> p t h d", t=TILES, d=XDIM),
                    bv_row[:].rearrange("p (o h d) -> p o h d", o=1, d=XDIM).to_broadcast([P, TILES, XHEADS, XDIM]),
                    ALU.add).then_inc(xv_out.sem, 1)

                def maxima(h):
                    wait(dve, xs_mm, b, h + 1)
                    if h >= 4:
                        wait(dve, x_exp, b, 2 * (h - 3))
                    nc.vector.tensor_reduce(xmax[:, h % 4, :], bank(h % 4).rearrange("p (t k) -> p t k", t=TILES),
                                            AX.X, ALU.max).then_inc(x_max.sem, 1)
                    wait(dve, x_max, b, h + 1)
                    nc.vector.tensor_scalar(xneg[:, h % 4, :], xmax[:, h % 4, :], -float(XDIM) ** -0.5, None, ALU.mult)\
                        .then_inc(x_neg.sem, 1)

                def outputs(m):
                    wait(dve, xo_mm, b, PER * (m + 1))
                    if m:
                        wait(dve, xon_done, b, m)
                    nc.vector.tensor_copy(xo[:], bank(6 + m % 2)[:, 0:SEQ]).then_inc(xo_out.sem, 1)
                    wait(dve, xsum_mm, b, m + 1)
                    nc.vector.reciprocal(xrec[:], bank(6 + m % 2)[:, SEQ:2 * SEQ]).then_inc(xrec_done.sem, 1)
                    wait(dve, xrec_done, b, m + 1)
                    nc.vector.tensor_tensor(xon[:, m, :], xo[:], xrec[:], ALU.mult).then_inc(xon_done.sem, 1)

                for h in range(XHEADS + 3):
                    if h < XHEADS:
                        maxima(h)
                    if h >= 6 and (h - 6) % PER == 0:
                        outputs((h - 6) // PER)
                wait(dve, xy_mm, b)
                nc.vector.tensor_scalar(xtmp[:], bank(4)[:, 0:SEQ], bxo[:, 0:1], tgate[:, 0:1], ALU.add, ALU.mult)\
                    .then_inc(xy_scaled.sem, 1)
                wait(dve, xy_scaled, b)
                nc.vector.tensor_tensor(x2T[:, bs], xtmp[:], xT[:, bs], ALU.add).then_inc(xy_done.sem, 1)

            dve.wait_ge(xy_done.sem, BATCH)
            big_norm(x2T[:], xT[:], 5, (DVE_C2, 5)).then_inc(x_ready.sem, 1)

            def halves(ap, half):
                return ap.rearrange("p (k h d) -> p k h d", k=2, d=HDIM)[:, :, :, 32 * half:32 * half + 32]

            def lengths(n, t):
                wait(dve, squared, n, 2 * t + 2)
                nc.vector.tensor_reduce(norm2[:, t, :], squares[:].rearrange("p (h d) -> p h d", d=HDIM), AX.X, ALU.add)\
                    .then_inc(norm2_done.sem, 1)

            def inverses(n, t):
                wait(dve, norm_done, n, t + 1)
                nc.vector.tensor_scalar(norm_c[:, t, :], norm[:, t, :], 1e-12, None, ALU.max).then_inc(normc_done.sem, 1)
                wait(dve, normc_done, n, t + 1)
                nc.vector.reciprocal(inv_norm[:, t, :], norm_c[:, t, :]).then_inc(inv_done.sem, 1)

            def sines(n, t, first=False):
                layer = n // BATCH
                wait(dve, qkv_copied, n, 3 * t + 2)
                if t:
                    wait(dve, qk_done, n, 1)
                elif not first:
                    wait(dve, qk_done, n - 1)
                for half in range(2):
                    table = rot_sin[:, bass.ds(layer * TILES + t, 1), :].rearrange("p o (k h d) -> p (o k) h d", k=2, h=1)
                    nc.vector.tensor_tensor(
                        halves(by_sin[:], half), halves(raw[:, t, :], 1 - half),
                        table[:, :, :, 32 * half:32 * half + 32].to_broadcast([P, 2, HEADS, 32]), ALU.mult)\
                        .then_inc(sin_done.sem, 1)

            def rotate(n, t):
                wait(dve, sin_done, n, 2 * t + 2)
                wait(dve, cos_done, n, t + 1)
                nc.vector.tensor_tensor(by_sin[:], by_sin[:], by_cos[:], ALU.add).then_inc(rot_done.sem, 1)
                wait(dve, rot_done, n, t + 1)
                wait(dve, inv_done, n, t + 1)
                nc.vector.tensor_tensor(
                    raw[:, t, :].rearrange("p (h d) -> p h d", d=HDIM), by_sin[:].rearrange("p (h d) -> p h d", d=HDIM),
                    inv_norm[:, t, :].rearrange("p (h o) -> p h o", o=1).to_broadcast([P, 2 * HEADS, HDIM]), ALU.mult)\
                    .then_inc(qk_done.sem, 1)

            def heads_split(ap):
                return ap.rearrange("p (a o d) -> p o a d", o=2, d=64)

            def shift(n, t):
                wait(dve, s_mm, n, t + 1)
                ps = pe_lo[t][:].rearrange("p (o a d) -> p o a d", o=2, d=64)
                nc.vector.tensor_reduce(row_max[:, t, :], pe_lo[t][:].rearrange("p (h d) -> p h d", d=64), AX.X, ALU.max)\
                    .then_inc(max_done.sem, 1)
                wait(dve, max_done, n, t + 1)
                nc.vector.tensor_tensor(
                    heads_split(probs[:, t, :]), ps,
                    row_max[:, t, :].rearrange("p (o a d) -> p o a d", o=2, d=1).to_broadcast([P, 2, PAIRS, 64]),
                    ALU.subtract).then_inc(shifted.sem, 1)

            def sums(n, t):
                wait(dve, exp_done, n, t + 1)
                nc.vector.tensor_reduce(row_sum[:, t, :], probs[:, t, :].rearrange("p (h d) -> p h d", d=64), AX.X, ALU.add)\
                    .then_inc(sum_done.sem, 1)
                wait(dve, sum_done, n, t + 1)
                nc.vector.reciprocal(row_inv[:, t, :], row_sum[:, t, :]).then_inc(rinv_done.sem, 1)

            def take_att(n, t):
                wait(dve, pv_mm, n, t + 1)
                wait(dve, rinv_done, n, t + 1)
                nc.vector.tensor_tensor(
                    heads_split(att[:, t, :]), pe_hi[t][:].rearrange("p (o a d) -> p o a d", o=2, d=64),
                    row_inv[:, t, :].rearrange("p (a o d) -> p o a d", o=2, d=1).to_broadcast([P, 2, PAIRS, 64]),
                    ALU.mult).then_inc(att_done.sem, 1)

            def attend_end(n):
                bs0 = (n % BATCH) * SEQ
                wait(dve, y_mm, n)
                nc.vector.tensor_tensor(xfT[0:64, :], xT[0:64, bass.ds(bs0, SEQ)], bank(4)[0:64, 0:SEQ], ALU.add)\
                    .then_inc(x1_done.sem, 1)
                nc.vector.tensor_tensor(xfT[64:P, 1:SEQ], xT[64:P, bass.ds(bs0, SEQ - 1)], bank(4)[64:P, 0:SEQ - 1], ALU.add)\
                    .then_inc(x1_done.sem, 1)
                nc.vector.tensor_tensor(x1T[:], xT[:, bass.ds(bs0, SEQ)], bank(4)[:, 0:SEQ], ALU.add)\
                    .then_inc(x1_done.sem, 1)
                wait(dve, mean_mm, n)
                wait(dve, x1_done, n)
                nc.vector.tensor_tensor(centred[:], xfT[:], bank(5)[:, 0:SEQ], ALU.subtract).then_inc(centre_done.sem, 1)
                wait(dve, std_done, n)
                nc.vector.reciprocal(rstd[:], std[:]).then_inc(rstd_done.sem, 1)
                wait(dve, centre_done, n)
                wait(dve, rstd_done, n)
                nc.vector.tensor_tensor(normed[:], centred[:], rstd[:], ALU.mult).then_inc(normed_done.sem, 1)
                wait(dve, normed_done, n)
                dve.wait_ge(small_loaded, (n // BATCH + 1) * (16 * SMALLS))
                nc.vector.tensor_scalar(ffn_in[:], normed[:], ln_gb[:, 0:1], ln_gb[:, 1:2], ALU.mult, ALU.add)\
                    .then_inc(ffnin_done.sem, 1)
                wait(dve, up_mm, n)
                for j, (f0, fs) in enumerate(CHUNKS):
                    wait(dve, gelu_done, n, j + 1)
                    src = bank(5)[0:fs, SEQ * j:SEQ * j + SEQ] if j < 2 else bank(6)[0:fs, 0:SEQ]
                    nc.vector.scalar_tensor_tensor(hidden[0:fs, j, :], src, b_1[0:fs, 0, j:j + 1], gelu[0:fs, j, :],
                                                   ALU.add, ALU.mult).then_inc(hid_done.sem, 1)
                wait(dve, down_mm, n)
                nc.vector.scalar_tensor_tensor(xT[:, bass.ds(bs0, SEQ)], bank(7)[:, 0:SEQ], b_2[:, 0:1], x1T[:],
                                               ALU.add, ALU.add).then_inc(x_ready.sem, 1)

            for t in range(TILES):
                lengths(0, t)
            dve.wait_ge(pre_pool, POOL_ALL)
            for t in range(TILES):
                inverses(0, t)
                sines(0, t, first=True)
                rotate(0, t)
            with dve.Fori(0, STEPS - 1) as n:
                shift(n, 0)
                shift(n, 1)
                sums(n, 0)
                sums(n, 1)
                lengths(n + 1, 0)
                sines(n + 1, 0)
                inverses(n + 1, 0)
                rotate(n + 1, 0)
                lengths(n + 1, 1)
                sines(n + 1, 1)
                take_att(n, 0)
                take_att(n, 1)
                inverses(n + 1, 1)
                rotate(n + 1, 1)
                attend_end(n)
            shift(STEPS - 1, 0)
            shift(STEPS - 1, 1)
            sums(STEPS - 1, 0)
            sums(STEPS - 1, 1)
            take_att(STEPS - 1, 0)
            take_att(STEPS - 1, 1)
            attend_end(STEPS - 1)

            wait(dve, x_ready, STEPS - 1)
            nc.vector.scalar_tensor_tensor(x2T[:], xT[:], tgate[:, 1:2], x2T[:], ALU.mult, ALU.add).then_inc(fin_done, 1)


def _laid_out(i):
    import numpy as np

    f32 = np.float32

    def by_group(a, axis):
        shape = a.shape[:axis] + (XHEADS, GROUP) + a.shape[axis + 1:]
        spread = np.zeros(shape, f32)
        at = (slice(None),) * axis + (slice(None), slice(0, XDIM))
        spread[at] = a.reshape(a.shape[:axis] + (XHEADS, XDIM) + a.shape[axis + 1:])
        return spread

    def by_chunk(a):
        padded = np.zeros(a.shape[:1] + (len(CHUNKS) * P,) + a.shape[2:], f32)
        padded[:, 0:FFN] = a
        return padded

    xcolumns = np.concatenate([by_group(i["L0_xattn_bq"], 0).reshape(MGROUPS, P).T,
                               by_group(i["L0_xattn_bk"], 0).reshape(MGROUPS, P).T,
                               i["L0_xattn_bo"].reshape(P, 1)], 1)
    b1 = i["L0_ffn_b1"]
    columns = np.concatenate([by_chunk(b1[:, 0:FFN]).reshape(DEPTH, len(CHUNKS), P),
                              by_chunk(b1[:, FFN:]).reshape(DEPTH, len(CHUNKS), P),
                              i["L0_ffn_ln_g"].reshape(DEPTH, 1, P), i["L0_ffn_ln_b"].reshape(DEPTH, 1, P),
                              i["L0_ffn_b2"].reshape(DEPTH, 1, P)], 1).transpose(0, 2, 1)
    return {
        "x": i["x"], "ctx": i["ctx_1024"], "mask": i["mask_BxS2_bf0"],
        "g_xattn": i["g_xattn"], "g_ffn": i["g_ffn"],
        "Wq": by_group(i["L0_xattn_Wq"], 1), "Wk": by_group(i["L0_xattn_Wk"], 1), "Wv": i["L0_xattn_Wv"],
        "Wxo": by_group(i["L0_xattn_Wo"], 0).reshape(MGROUPS, P, DIM).transpose(1, 0, 2),
        "bv": i["L0_xattn_bv"], "xcolumns": xcolumns,
        "Wqkv": i["L0_ffn_Wqkv"], "q_scale": i["L0_ffn_q_scale"], "k_scale": i["L0_ffn_k_scale"],
        "Wo": i["L0_ffn_Wo"], "W1": i["L0_ffn_W1"], "W2": by_chunk(i["L0_ffn_W2"]), "columns": columns,
    }


def _shape_tables():
    import numpy as np

    f32 = np.float32
    half = np.arange(0, HDIM, 2, dtype=f32)
    t = np.arange(SEQ, dtype=f32)
    freqs = t[:, None] * (f32(1.0) / f32(10000.0) ** (half / f32(HDIM)))[None, :]
    scale = ((half + f32(0.4 * HDIM)) / f32(1.4 * HDIM))[None, :] ** ((t - SEQ // 2) / f32(WIN // 2))[:, None]
    two = lambda a: np.concatenate([a, a], -1)
    cos, sin, scale = two(np.cos(freqs)), np.concatenate([-np.sin(freqs), np.sin(freqs)], -1), two(scale)
    a, j = np.arange(WIN)[:, None], np.arange(2 * WIN)[None, :]
    seen = np.where(j < WIN, j >= a, j - WIN <= a)
    hidden = np.tile(np.where(seen, 0.0, -1e30), (WINDOWS, 1))
    hidden[:WIN, :WIN] = -1e30
    p = np.arange(P)
    ones_row = (p % GROUP == XDIM).astype(f32)
    return {
        "t_cos": np.concatenate([cos * scale, cos / scale], -1).astype(f32),
        "t_sin": np.concatenate([sin * scale, sin / scale], -1).astype(f32),
        "t_mask": hidden.astype(f32),
        "t_ident": np.eye(P, dtype=f32),
        "t_spread": ((p[:, None] // GROUP == p[None, :] // GROUP) * ones_row[:, None]).astype(f32),
        "t_maskrow": ones_row[None, :],
        "t_one": ones_row[:, None],
    }


def kernel(**inputs):
    import numpy as _np
    import concourse.bacc as _bacc
    from concourse import mybir as _mybir
    from concourse.bass_utils import run_bass_kernel_spmd as _run

    nc = _bacc.Bacc("TRN2", target_bir_lowering=False, num_devices=1)
    arrays, args = {}, []
    given = _laid_out({name: _np.asarray(a) for name, a in inputs.items()}) | _shape_tables()
    for name, a in given.items():
        arrays[f"in_{name}_dram"] = a = _np.ascontiguousarray(a)
        args.append(nc.dram_tensor(f"in_{name}_dram", a.shape, _mybir.dt.from_np(a.dtype), kind="ExternalInput").ap())
    out = nc.dram_tensor("out_0_dram", (BATCH, SEQ, DIM), _mybir.dt.float32, kind="ExternalOutput").ap()
    build(nc, *args, out)
    r = _run(nc, [arrays], core_ids=[0])
    return r.results[0]["out_0_dram"]
```

```python
from contextlib import ExitStack

import concourse.bass as bass
from concourse import mybir

ALU = mybir.AluOpType
ACT = mybir.ActivationFunctionType
AX = mybir.AxisListType
F32 = mybir.dt.float32
BF16 = mybir.dt.bfloat16
U8 = mybir.dt.uint8

P = 128
BATCH, SEQ, DIM = 4, 256, 128
TILES = SEQ // P
TOKENS = BATCH * SEQ
XHEADS = 16
XDIM = DIM // XHEADS
GROUP = 32
PER = P // GROUP
MGROUPS = XHEADS // PER
DEPTH = 6
HEADS, HDIM, WIN = 16, 64, 32
INNER = HEADS * HDIM
PAIRS = HEADS // 2
QUADS = P // WIN
WINDOWS = SEQ // WIN
STEPS = DEPTH * BATCH
QK_SCALE = 8.0
FFN = DIM * 4 * 2 // 3
CHUNKS = [(0, 128), (128, 128), (256, FFN - 256)]
V_MOVES = 4 * QUADS
LCOLS = 2 * len(CHUNKS) + 3


class Signal:

    def __init__(self, sem, per=1, before=0):
        self.sem, self.per, self.before = sem, per, before

    def upto(self, n, k=None):
        return n * self.per + (self.before + (self.per if k is None else k))


def build(nc, x, ctx, mask, g_xattn, g_ffn, Wq, Wk, Wv, Wxo, bv, xcolumns,
          Wqkv, q_scale, k_scale, Wo, W1, W2, columns,
          t_cos, t_sin, t_mask, t_ident, t_spread, t_headrows, out):
    DVE_XT, DVE_CT, DVE_C1, DVE_LN1, DVE_C2 = 11, 12, 13, 15, 16
    POOL_CONST, POOL_ALL = 4, 14
    with ExitStack() as stack:
        def sb(name, shape, dt=F32):
            return stack.enter_context(nc.sbuf_tensor(name, shape, dt))

        def sem(name):
            return stack.enter_context(nc.semaphore(name))

        ident = sb("ident", [P, P])
        ident_bf = sb("ident_bf", [P, P], BF16)
        window_mask_f = sb("window_mask_f", [P, TILES, 64])
        window_mask = sb("window_mask", [P, TILES, 8, 64], BF16)
        mean_of = sb("mean_of", [P, P])
        eps = sb("eps", [P, 1])
        spread = sb("spread", [P, P])
        head_rows = sb("head_rows", [P, XHEADS])
        x_in = sb("x_in", [P, BATCH * TILES, DIM])
        mask_u8 = sb("mask_u8", [1, TOKENS], U8)
        mask_top = sb("mask_top", [P, TOKENS], BF16)
        ones_top = sb("ones_top", [P, P], BF16)
        gates = sb("gates", [P, 2])
        tgate = sb("tgate", [P, 2])

        xT = sb("xT", [P, TOKENS])
        x2T = sb("x2T", [P, TOKENS])

        wv_in = sb("wv_in", [P, DIM])
        wxo_pad = sb("wxo_pad", [P, MGROUPS, DIM])
        xcol = sb("xcol", [P, 3])
        bq, bk, bxo = xcol[:, 0:1], xcol[:, 1:2], xcol[:, 2:3]
        bv_row = sb("bv_row", [P, DIM])
        q_here = sb("q_here", [P, SEQ])
        xmax = sb("xmax", [P, 4, TILES])
        xneg = sb("xneg", [P, 4, TILES])
        xo = sb("xo", [P, SEQ])
        xrec = sb("xrec", [P, SEQ])
        xtmp = sb("xtmp", [P, SEQ])

        w_qkv = sb("w_qkv", [P, 3 * INNER])
        w_o = sb("w_o", [P, PAIRS, DIM])
        w_1 = sb("w_1", [P, 2 * FFN])
        w_2 = sb("w_2", [P, len(CHUNKS), DIM])
        lcol = sb("lcol", [P, LCOLS])
        b_1 = lcol[:, 0:6].rearrange("p (h c) -> p h c", h=2)
        ln_gb, b_2 = lcol[:, 6:8], lcol[:, 8:9]
        cos_in = sb("cos_in", [P, TILES, 2 * HDIM])
        sin_in = sb("sin_in", [P, TILES, 2 * HDIM])
        scales = sb("scales", [P, DEPTH, 2 * HDIM])
        rot_cos = sb("rot_cos", [P, DEPTH * TILES, 2 * HDIM])
        rot_sin = sb("rot_sin", [P, DEPTH * TILES, 2 * HDIM])

        xs = sb("xs", [P, SEQ])
        raw = sb("raw", [P, TILES, 2 * INNER])
        squares = sb("squares", [P, 2 * INNER])
        by_cos = sb("by_cos", [P, 2 * INNER])
        by_sin = sb("by_sin", [P, 2 * INNER])
        norm2 = sb("norm2", [P, TILES, 2 * HEADS])
        norm = sb("norm", [P, TILES, 2 * HEADS])
        norm_c = sb("norm_c", [P, TILES, 2 * HEADS])
        inv_norm = sb("inv_norm", [P, TILES, 2 * HEADS])
        v_tok = sb("v_tok", [P, TILES, INNER])
        v_win = sb("v_win", [P, WINDOWS, INNER // 2])
        qkT = sb("qkT", [P, 2 * PAIRS, SEQ])

        row_max = sb("row_max", [P, TILES, HEADS])
        row_sum = sb("row_sum", [P, TILES, HEADS])
        row_inv = sb("row_inv", [P, TILES, HEADS])
        probs = sb("probs", [P, TILES, HEADS * 64])
        probsT = sb("probsT", [P, TILES, PAIRS * P])
        att = sb("att", [P, TILES, INNER])
        attT = sb("attT", [P, PAIRS, SEQ])
        x1T = sb("x1T", [P, SEQ])
        xfT = sb("xfT", [P, SEQ])
        ln_big = by_sin
        centred = sb("centred", [P, SEQ])
        centred2 = sb("centred2", [P, SEQ])
        std = sb("std", [P, SEQ])
        rstd = sb("rstd", [P, SEQ])
        normed = sb("normed", [P, SEQ])
        ffn_in = sb("ffn_in", [P, SEQ])
        gelu = sb("gelu", [P, len(CHUNKS), SEQ])
        hidden = sb("hidden", [P, len(CHUNKS), SEQ])

        c_in = att[:, 0, :].rearrange("p (a d) -> p a d", d=DIM)
        xon = att[:, 1, :].rearrange("p (m s) -> p m s", m=MGROUPS)
        wq, wk = attT[:, 0, 0:DIM], attT[:, 1, 0:DIM]
        v_aug = attT[:, 4:8, :].rearrange("p a s -> p (a s)").rearrange("p (t h g) -> p t h g", t=TILES, g=GROUP)
        xn_big = by_cos[:, 0:TOKENS]
        sq_big = by_cos[:, TOKENS:2 * TOKENS]
        sd_big = ln_big[:, 0:TOKENS]
        rs_big = ln_big[:, TOKENS:2 * TOKENS]
        cT = squares[:, 0:TOKENS]
        xnT = squares[:, TOKENS:2 * TOKENS]
        q_all, k_all = raw[:, 0, 0:TOKENS], raw[:, 0, TOKENS:2 * TOKENS]
        v_all = v_tok[:, 1, :].rearrange("p (t h d) -> p t h d", h=XHEADS, d=XDIM)
        q_head = qkT
        p_x = raw[:, 1, :].rearrange("p (r q k) -> p r q k", r=4, q=TILES)
        pT_x = v_tok[:, 0, :].rearrange("p (r k q) -> p r k q", r=2, k=TILES)

        pe_lo = [stack.enter_context(nc.psum_tensor(f"ps_s{i}", [P, 1024], F32)) for i in range(2)]
        pe_hi = [stack.enter_context(nc.psum_tensor(f"ps_g{i}", [P, 1024], F32)) for i in range(2)]

        FILLS = [(0, 0), (0, 1), (1, 0), (1, 1), (0, 2), (1, 2)]
        FILL = pe_hi[0]

        def bank(i):
            t = (pe_lo + pe_hi)[i // 2]
            return t[:, 512 * (i % 2):512 * (i % 2) + 512]

        loaded = sem("loaded")
        pre_dve = sem("pre_dve")
        pre_pool = sem("pre_pool")
        pre_act = sem("pre_act")
        pre_pe = sem("pre_pe")
        qkv_all_mm = sem("qkv_all_mm")
        qkv_all_out = sem("qkv_all_out")
        q_taken = Signal(sem("q_taken"))
        q_headed = Signal(sem("q_headed"), XHEADS)
        xv_out = Signal(sem("xv_out"))
        xs_mm = Signal(sem("xs_mm"), XHEADS)
        x_max = Signal(sem("x_max"), XHEADS)
        x_neg = Signal(sem("x_neg"), XHEADS)
        x_exp = Signal(sem("x_exp"), 2 * XHEADS)
        xt_mm = Signal(sem("xt_mm"), XHEADS)
        xt_out = Signal(sem("xt_out"), XHEADS)
        xo_mm = Signal(sem("xo_mm"), XHEADS)
        xo_out = Signal(sem("xo_out"), MGROUPS)
        xsum_mm = Signal(sem("xsum_mm"), MGROUPS)
        xrec_done = Signal(sem("xrec_done"), MGROUPS)
        xon_done = Signal(sem("xon_done"), MGROUPS)
        xy_mm = Signal(sem("xy_mm"))
        xy_scaled = Signal(sem("xy_scaled"))
        xy_done = Signal(sem("xy_done"))
        qk_loaded = sem("qk_loaded")
        v_loaded = sem("v_loaded")
        out_loaded = sem("out_loaded")
        small_loaded = sem("small_loaded")
        x_ready = Signal(sem("x_ready"), 1, 1)
        xs_ready = Signal(sem("xs_ready"), 2)
        qkv_mm = Signal(sem("qkv_mm"), 6)
        qkv_copied = Signal(sem("qkv_copied"), 6)
        squared = Signal(sem("squared"), 4)
        norm2_done = Signal(sem("norm2_done"), 2)
        norm_done = Signal(sem("norm_done"), 2)
        normc_done = Signal(sem("normc_done"), 2)
        inv_done = Signal(sem("inv_done"), 2)
        cos_done = Signal(sem("cos_done"), 2)
        sin_done = Signal(sem("sin_done"), 2)
        swung = Signal(sem("swung"), 2)
        rot_done = Signal(sem("rot_done"), 2)
        qk_done = Signal(sem("qk_done"), 2)
        qkT_mm = Signal(sem("qkT_mm"), 4)
        qkT_out = Signal(sem("qkT_out"), 4)
        v_moved = Signal(sem("v_moved"), 16 * V_MOVES)
        s_mm = Signal(sem("s_mm"), 2)
        max_done = Signal(sem("max_done"), 2)
        shifted = Signal(sem("shifted"), 2)
        exp_done = Signal(sem("exp_done"), 2)
        sum_done = Signal(sem("sum_done"), 2)
        rinv_done = Signal(sem("rinv_done"), 2)
        pT_mm = Signal(sem("pT_mm"), 2)
        pT_out = Signal(sem("pT_out"), 2)
        pv_mm = Signal(sem("pv_mm"), 2)
        att_done = Signal(sem("att_done"), 2)
        attT_mm = Signal(sem("attT_mm"), 2)
        attT_out = Signal(sem("attT_out"), 2)
        y_mm = Signal(sem("y_mm"))
        x1_done = Signal(sem("x1_done"), 3)
        mean_mm = Signal(sem("mean_mm"))
        centre_done = Signal(sem("centre_done"))
        csq_done = Signal(sem("csq_done"))
        var_mm = Signal(sem("var_mm"))
        std_done = Signal(sem("std_done"))
        rstd_done = Signal(sem("rstd_done"))
        normed_done = Signal(sem("normed_done"))
        ffnin_done = Signal(sem("ffnin_done"))
        gate_mm = Signal(sem("gate_mm"), 2)
        up_mm = Signal(sem("up_mm"))
        gelu_done = Signal(sem("gelu_done"), 3)
        hid_done = Signal(sem("hid_done"), 3)
        down_mm = Signal(sem("down_mm"))
        fin_done = sem("fin_done")
        fin_mm = sem("fin_mm")
        fin_copied = sem("fin_copied")
        stored = sem("stored")

        def token_tiles(a):
            return a.rearrange("b (t p) d -> p (b t) d", p=P)

        def halves(ap, half):
            return ap.rearrange("p (k h d) -> p k h d", k=2, d=HDIM)[:, :, :, 32 * half:32 * half + 32]

        def sine_half(engine, n, t, half):
            table = rot_sin[:, bass.ds(n // BATCH * TILES + t, 1), :].rearrange("p o (k h d) -> p (o k) h d", k=2, h=1)
            return engine.tensor_tensor(
                halves(by_sin[:], half), halves(raw[:, t, :], 1 - half),
                table[:, :, :, 32 * half:32 * half + 32].to_broadcast([P, 2, HEADS, 32]), ALU.mult)

        LOADS = []

        def later(n):
            return not isinstance(n, int) or n > 0

        def run(stage, n, *args):
            if not isinstance(n, int) or 0 <= n < STEPS:
                stage(n, *args)

        def wait(engine, signal, n, k=None):
            engine.wait_ge(signal.sem, signal.upto(n, k))

        block = stack.enter_context(nc.Block())

        @block.sync
        def _(sp):
            def load(dst, src):
                LOADS.append(1)
                sp.dma_start(dst, src).then_inc(loaded, 16)

            load(ident[:], t_ident)
            load(x_in[:], token_tiles(x))
            load(c_in, token_tiles(ctx))
            load(wq, Wq)
            load(wk, Wk)
            load(wxo_pad[:], Wxo)
            load(xcol[:], xcolumns)
            load(wv_in[:], Wv)
            load(mask_u8[:], mask.rearrange("(o b) s -> o (b s)", o=1))
            load(gates[:, 0:1], g_xattn.rearrange("(o d) -> o d", o=1).partition_broadcast(P))
            load(gates[:, 1:2], g_ffn.rearrange("(o d) -> o d", o=1).partition_broadcast(P))
            load(bv_row[:], bv.rearrange("(o d) -> o d", o=1).partition_broadcast(P))
            load(spread[:], t_spread)
            load(head_rows[:], t_headrows)
            load(cos_in[:], t_cos.rearrange("(t p) d -> p t d", p=P))
            load(sin_in[:], t_sin.rearrange("(t p) d -> p t d", p=P))
            load(window_mask_f[:], t_mask.rearrange("(t p) d -> p t d", p=P))
            load(scales[:, :, 0:HDIM], q_scale.rearrange("(o l) d -> o l d", o=1).partition_broadcast(P))
            load(scales[:, :, HDIM:], k_scale.rearrange("(o l) d -> o l d", o=1).partition_broadcast(P))
            def load_qk(layer):
                sp.dma_start(w_qkv[:, 0:2 * INNER], Wqkv[layer, :, 0:2 * INNER]).then_inc(qk_loaded, 16)

            def load_v(layer):
                sp.dma_start(w_qkv[:, 2 * INNER:], Wqkv[layer, :, 2 * INNER:]).then_inc(v_loaded, 16)

            def load_out(layer):
                sp.dma_start(w_o[:], Wo[layer].rearrange("(c p) d -> p c d", p=P)).then_inc(out_loaded, 16)

            def load_small(layer):
                sp.dma_start(w_1[:], W1[layer]).then_inc(small_loaded, 16)
                sp.dma_start(w_2[:], W2[layer].rearrange("(c p) d -> p c d", p=P)).then_inc(small_loaded, 16)
                sp.dma_start(lcol[:], columns[layer]).then_inc(small_loaded, 16)

            def move_values(n, first=False):
                wait(sp, qkv_copied, n)
                if not first:
                    wait(sp, pv_mm, n - 1)
                for odd in range(2):
                    cols = slice(512 * odd, 512 * odd + 512)
                    for c in range(QUADS):
                        src = v_tok[WIN * c:WIN * c + WIN, :, cols]
                        own = slice(64 * odd + 32, 64 * odd + 64)
                        before = slice(64 * odd, 64 * odd + 32)
                        sp.dma_start(v_win[own, c:WINDOWS:QUADS, :], src).then_inc(v_moved.sem, 16)
                        if c < QUADS - 1:
                            sp.dma_start(v_win[before, c + 1:WINDOWS:QUADS, :], src).then_inc(v_moved.sem, 16)
                        else:
                            sp.dma_start(v_win[before, QUADS, :], src[:, 0]).then_inc(v_moved.sem, 16)

            load_qk(0)
            load_v(0)
            load_out(0)
            load_small(0)
            move_values(0, first=True)
            with sp.Fori(1, DEPTH) as layer:
                with sp.Fori(1, BATCH - 1) as j:
                    move_values(layer * BATCH + j - BATCH)
                wait(sp, qkv_mm, layer * BATCH - 1, 4)
                load_qk(layer)
                move_values(layer * BATCH - 1)
                load_v(layer)
                move_values(layer * BATCH)
                wait(sp, y_mm, layer * BATCH - 1)
                load_out(layer)
                wait(sp, x_ready, layer * BATCH - 1)
                load_small(layer)
            with sp.Fori(STEPS - BATCH + 1, STEPS) as n:
                move_values(n)

            sp.wait_ge(fin_copied, 1)
            sp.dma_start(token_tiles(out), x_in[:]).then_inc(stored, 16)
            sp.wait_ge(stored, 16)

        n_loads = len(LOADS)
        SMALLS = 3

        @block.gpsimd
        def _(pool):
            nc.gpsimd.memset(v_aug, 0.0).then_inc(pre_pool, 1)
            pool.wait_ge(pre_pool, 1)
            nc.gpsimd.memset(v_aug[:, :, :, XDIM:XDIM + 1], 1.0).then_inc(pre_pool, 1)
            nc.gpsimd.memset(mean_of[:], 1.0 / DIM).then_inc(pre_pool, 1)
            nc.gpsimd.memset(eps[:], 1e-5).then_inc(pre_pool, 1)
            pool.wait_ge(loaded, 16 * n_loads)
            for t in range(TILES):
                nc.gpsimd.tensor_tensor(rot_cos[:, t::TILES, :], cos_in[:, t:t + 1, :].to_broadcast([P, DEPTH, 2 * HDIM]),
                                        scales[:], ALU.mult).then_inc(pre_pool, 1)
                for qk in range(2):
                    for half in range(2):
                        d = HDIM * qk + 32 * half
                        o = HDIM * qk + 32 * (1 - half)
                        nc.gpsimd.tensor_tensor(rot_sin[:, t::TILES, d:d + 32],
                                                sin_in[:, t:t + 1, d:d + 32].to_broadcast([P, DEPTH, 32]),
                                                scales[:, :, o:o + 32], ALU.mult).then_inc(pre_pool, 1)

            def head_queries(b, first=False):
                if not first:
                    wait(pool, q_headed, b - 1)
                nc.gpsimd.tensor_copy(q_here[:], q_all[:, bass.ds(b * SEQ, SEQ)]).then_inc(q_taken.sem, 1)
                wait(pool, q_taken, b)
                for h in range(XHEADS):
                    if not first:
                        wait(pool, xs_mm, b - 1, h + 1)
                    nc.gpsimd.tensor_tensor(q_head[:, h, :], q_here[:], head_rows[:, h:h + 1].to_broadcast([P, SEQ]),
                                            ALU.mult).then_inc(q_headed.sem, 1)

            pool.wait_ge(qkv_all_out, 3)
            head_queries(0, first=True)
            with pool.Fori(1, BATCH) as b:
                head_queries(b)

            def shift_x(n, upto):
                wait(pool, x_ready, upto)
                if later(n):
                    wait(pool, qkv_mm, n - 1)
                    wait(pool, cos_done, n - 1)
                    wait(pool, swung, n - 1)
                b = n % BATCH
                nc.gpsimd.tensor_copy(xs[0:64, :], xT[0:64, bass.ds(b * SEQ, SEQ)]).then_inc(xs_ready.sem, 1)
                wait(pool, xs_ready, n, 1)
                nc.gpsimd.tensor_copy(xs[64:P, 1:SEQ], xT[64:P, bass.ds(b * SEQ, SEQ - 1)]).then_inc(xs_ready.sem, 1)
                wait(pool, xs_ready, n)

            def cosines(n, t):
                layer = n // BATCH
                wait(pool, qkv_copied, n, 2 * t + 2)
                if t:
                    wait(pool, rot_done, n, 1)
                elif later(n):
                    wait(pool, rot_done, n - 1)
                nc.gpsimd.tensor_tensor(
                    by_cos[:].rearrange("p (k h d) -> p k h d", k=2, d=HDIM),
                    raw[:, t, :].rearrange("p (k h d) -> p k h d", k=2, d=HDIM),
                    rot_cos[:, bass.ds(layer * TILES + t, 1), :].rearrange("p o (k h d) -> p (o k) h d", k=2, h=1)
                    .to_broadcast([P, 2, HEADS, HDIM]), ALU.mult).then_inc(cos_done.sem, 1)

            def swing(n, t):
                if t:
                    wait(pool, qk_done, n, 1)
                elif later(n):
                    wait(pool, qk_done, n - 1)
                sine_half(nc.gpsimd, n, t, 0).then_inc(swung.sem, 1)

            def prepare(n, upto):
                shift_x(n, upto)
                for t in range(TILES):
                    cosines(n, t)
                    swing(n, t)

            for n in range(BATCH):
                prepare(n, -1)
            with pool.Fori(BATCH, STEPS) as n:
                prepare(n, n - BATCH)

        @block.tensor
        def _(pe):
            pe.wait_ge(loaded, 16 * n_loads)
            for i in range(BATCH * TILES):
                mm = nc.tensor.transpose(pe_lo[0][:, P * i:P * i + P], x_in[:, i, :], ident[:])
            mm.then_inc(pre_pe, 1)
            for i in range(BATCH * TILES):
                mm = nc.tensor.transpose(pe_lo[1][:, P * i:P * i + P], c_in[:, i, :], ident[:])
            mm.then_inc(pre_pe, 1)

            def big_mean(src, out_ps):
                for j in range(2):
                    mm = nc.tensor.matmul(out_ps[:, 512 * j:512 * j + 512], mean_of[:], src[:, 512 * j:512 * j + 512],
                                          start=True, stop=True)
                mm.then_inc(pre_pe, 1)

            pe.wait_ge(pre_dve, DVE_XT)
            pe.wait_ge(pre_pool, POOL_CONST)
            big_mean(xT, pe_hi[0])

            def project_all(w, src, out_ps):
                for j in range(2):
                    mm = nc.tensor.matmul(out_ps[:, 512 * j:512 * j + 512], w, src[:, 512 * j:512 * j + 512],
                                          start=True, stop=True)
                mm.then_inc(qkv_all_mm, 1)

            pe.wait_ge(pre_dve, DVE_CT)
            project_all(wk, cT, pe_lo[1])
            for i in range(BATCH * TILES):
                mm = nc.tensor.matmul(pe_lo[0][:, P * i:P * i + P], cT[:, P * i:P * i + P], wv_in[:], start=True, stop=True)
            mm.then_inc(qkv_all_mm, 1)
            pe.wait_ge(pre_act, 2)
            big_mean(sq_big, pe_hi[1])
            pe.wait_ge(pre_dve, DVE_LN1)
            project_all(wq, xnT, pe_hi[0])

            pe.wait_ge(qkv_all_out, 3)
            with pe.Fori(0, BATCH) as b:
                bs = bass.ds(b * SEQ, SEQ)

                def scores(h):
                    wait(pe, q_headed, b, h + 1)
                    if h >= 4:
                        wait(pe, x_exp, b, 2 * (h - 3))
                    for t in range(TILES):
                        nc.tensor.matmul(bank(h % 4)[:, SEQ * t:SEQ * t + SEQ], ones_top[:], mask_top[:, bs],
                                         start=True, stop=False)
                        mm = nc.tensor.matmul(bank(h % 4)[:, SEQ * t:SEQ * t + SEQ], q_head[:, h, P * t:P * t + P],
                                              k_all[:, bs], start=False, stop=True)
                    mm.then_inc(xs_mm.sem, 1)

                def turn(h):
                    wait(pe, x_exp, b, 2 * (h + 1))
                    if h >= 2:
                        wait(pe, xt_out, b, h - 1)
                    for k in range(TILES):
                        for t in range(TILES):
                            mm = nc.tensor.transpose(bank(4 + h % 2)[:, SEQ * k + P * t:SEQ * k + P * t + P],
                                                     p_x[:, h % 4, t, P * k:P * k + P], ident[:])
                    mm.then_inc(xt_mm.sem, 1)

                def values(h):
                    m, g = divmod(h, PER)
                    wait(pe, xt_out, b, h + 1)
                    if h == 0:
                        wait(pe, xv_out, b)
                    if g == 0 and m >= 2:
                        wait(pe, xrec_done, b, m - 1)
                    for k in range(TILES):
                        mm = nc.tensor.matmul(bank(6 + m % 2)[GROUP * g:GROUP * g + GROUP, 0:SEQ], v_aug[:, k, h, :],
                                              pT_x[:, h % 2, k, :], start=(k == 0), stop=(k == 1),
                                              tile_position=(0, GROUP * g))
                    mm.then_inc(xo_mm.sem, 1)

                def sums(m):
                    wait(pe, xo_out, b, m + 1)
                    nc.tensor.matmul(bank(6 + m % 2)[:, SEQ:2 * SEQ], spread[:], xo[:], start=True, stop=True)\
                        .then_inc(xsum_mm.sem, 1)

                for h in range(XHEADS + 4):
                    if h < XHEADS:
                        scores(h)
                    if 0 <= h - 2 < XHEADS:
                        turn(h - 2)
                    if 0 <= h - 3 < XHEADS:
                        values(h - 3)
                    if h >= 7 and (h - 7) % PER == 0:
                        sums((h - 7) // PER)
                wait(pe, xon_done, b)
                for m in range(MGROUPS):
                    mm = nc.tensor.matmul(bank(4)[:, 0:SEQ], wxo_pad[:, m, :], xon[:, m, :], start=(m == 0),
                                          stop=(m == MGROUPS - 1))
                mm.then_inc(xy_mm.sem, 1)
                wait(pe, xy_scaled, b)

            pe.wait_ge(xy_done.sem, BATCH)
            big_mean(x2T, pe_hi[0])
            pe.wait_ge(pre_act, 4)
            big_mean(sq_big, pe_hi[1])
            pe.wait_ge(x_ready.sem, 1)

            def project(n, i):
                t, part = FILLS[i]
                if i == 4:
                    pe.wait_ge(v_loaded, (n // BATCH + 1) * 16)
                if i:
                    wait(pe, qkv_copied, n, i)
                    if i < 5:
                        wait(pe, squared, n, i)
                else:
                    wait(pe, xs_ready, n)
                    pe.wait_ge(qk_loaded, (n // BATCH + 1) * 16)
                    if later(n):
                        wait(pe, qkv_copied, n - 1)
                for j in range(2):
                    if part < 2:
                        cols = w_qkv[:, INNER * part + 512 * j:INNER * part + 512 * j + 512]
                    else:
                        cols = w_qkv[:, 2 * INNER:].rearrange("p (h o d) -> p o h d", o=2, d=HDIM)[:, j]
                    mm = nc.tensor.matmul(FILL[:, 512 * j:512 * j + 512], xs[:, P * t:P * t + P], cols,
                                          start=True, stop=True)
                mm.then_inc(qkv_mm.sem, 1)

            def turn_qk(n, t, part):
                if part:
                    wait(pe, qkT_out, n, 2 * t + 1)
                else:
                    wait(pe, qk_done, n, t + 1)
                    if later(n):
                        wait(pe, att_done, n - 1, t + 1)
                for p in range(PAIRS):
                    mm = nc.tensor.transpose(pe_lo[t][:, P * p:P * p + P],
                                             raw[:, t, P * (PAIRS * part + p):P * (PAIRS * part + p) + P], ident[:])
                mm.then_inc(qkT_mm.sem, 1)

            def scores(n, t):
                wait(pe, qkT_out, n, 2 * t + 2)
                ps = pe_lo[t]
                for odd in range(2):
                    nc.tensor.matmul(ps[:, 512 * odd:512 * odd + 512], ident_bf[:], window_mask[:, t], start=True,
                                     stop=False, skip_group_check=True)
                for h in range(HEADS):
                    rows = slice(64 * (h % 2), 64 * (h % 2) + 64)
                    for c in range(QUADS):
                        w = QUADS * t + c
                        k0 = WIN * max(w - 1, 0)
                        keys = WIN * (w + 1) - k0
                        o = 512 * (h % 2) + 64 * (h // 2) + 64 - keys
                        mm = nc.tensor.matmul(ps[WIN * c:WIN * c + WIN, o:o + keys],
                                              qkT[rows, h // 2, WIN * w:WIN * w + WIN],
                                              qkT[rows, PAIRS + h // 2, k0:k0 + keys],
                                              start=False, stop=True, skip_group_check=True,
                                              tile_position=(64 * (h % 2), WIN * c))
                mm.then_inc(s_mm.sem, 1)

            def turn_probs(n, t):
                wait(pe, exp_done, n, t + 1)
                for p in range(PAIRS):
                    mm = nc.tensor.transpose(pe_lo[t][:, P * p:P * p + P], probs[:, t, P * p:P * p + P], ident[:])
                mm.then_inc(pT_mm.sem, 1)

            def weigh_values(n, t):
                wait(pe, pT_out, n, t + 1)
                wait(pe, v_moved, n)
                nc.tensor.matmul(pe_lo[t][:, 0:2], ident_bf[:], ident_bf[:, 0:2], start=True, stop=True)
                for h in range(HEADS):
                    odd = h % 2
                    for c in range(QUADS):
                        w = QUADS * t + c
                        r0 = 64 * odd + (32 if w == 0 else 0)
                        rows = slice(r0, 64 * odd + 64)
                        o = 512 * odd + 64 * (h // 2)
                        mm = nc.tensor.matmul(pe_lo[t][WIN * c:WIN * c + WIN, o:o + 64],
                                              probsT[rows, t, P * (h // 2) + WIN * c:P * (h // 2) + WIN * c + WIN],
                                              v_win[rows, w, 64 * (h // 2):64 * (h // 2) + 64],
                                              start=True, stop=True, skip_group_check=True,
                                              tile_position=(r0, WIN * c))
                mm.then_inc(pv_mm.sem, 1)

            def turn_att(n, half):
                if half:
                    wait(pe, attT_out, n, 1)
                else:
                    wait(pe, att_done, n)
                    wait(pe, x_ready, n - 1)
                for p in range(4):
                    for t in range(TILES):
                        mm = nc.tensor.transpose(pe_hi[1][:, SEQ * p + P * t:SEQ * p + P * t + P],
                                                 att[:, t, P * (4 * half + p):P * (4 * half + p) + P], ident[:])
                mm.then_inc(attT_mm.sem, 1)

            def out_project(n):
                wait(pe, attT_out, n)
                pe.wait_ge(out_loaded, (n // BATCH + 1) * 16)
                for p in range(PAIRS):
                    mm = nc.tensor.matmul(bank(6)[:, 0:SEQ], w_o[:, p, :], attT[:, p, :], start=(p == 0),
                                          stop=(p == PAIRS - 1))
                mm.then_inc(y_mm.sem, 1)

            def mean(n):
                wait(pe, x1_done, n)
                nc.tensor.matmul(bank(7)[:, 0:SEQ], mean_of[:], xfT[:], start=True, stop=True).then_inc(mean_mm.sem, 1)

            def variance(n):
                wait(pe, csq_done, n)
                nc.tensor.matmul(bank(6)[:, 0:SEQ], mean_of[:], centred2[:], start=True, stop=True).then_inc(var_mm.sem, 1)

            def ffn_bank(j, rows):
                return bank(7)[0:rows, SEQ * j:SEQ * j + SEQ] if j < 2 else bank(6)[0:rows, 0:SEQ]

            def gate(n):
                wait(pe, ffnin_done, n)
                pe.wait_ge(small_loaded, (n // BATCH + 1) * (16 * SMALLS))
                for j, (f0, fs) in enumerate(CHUNKS):
                    mm = nc.tensor.matmul(ffn_bank(j, fs), w_1[:, FFN + f0:FFN + f0 + fs], ffn_in[:],
                                          start=True, stop=True)
                    if j:
                        mm.then_inc(gate_mm.sem, 1)

            def up(n):
                for j, (f0, fs) in enumerate(CHUNKS):
                    wait(pe, gelu_done, n, max(j + 1, 2))
                    mm = nc.tensor.matmul(ffn_bank(j, fs), w_1[:, f0:f0 + fs], ffn_in[:], start=True, stop=True)
                mm.then_inc(up_mm.sem, 1)

            def down(n):
                wait(pe, hid_done, n)
                for j, (f0, fs) in enumerate(CHUNKS):
                    mm = nc.tensor.matmul(bank(7)[:, 0:SEQ], w_2[0:fs, j, :], hidden[0:fs, j, :], start=(j == 0),
                                          stop=(j == 2))
                mm.then_inc(down_mm.sem, 1)

            def turn(n):
                run(up, n - 2)
                run(turn_qk, n, 0, 0)
                run(project, n, 5)
                run(weigh_values, n - 1, 1)
                run(down, n - 2)
                run(turn_qk, n, 0, 1)
                run(project, n + 1, 0)
                run(turn_att, n - 1, 0)
                run(scores, n, 0)
                run(turn_att, n - 1, 1)
                run(project, n + 1, 1)
                run(turn_qk, n, 1, 0)
                run(out_project, n - 1)
                run(turn_probs, n, 0)
                run(turn_qk, n, 1, 1)
                run(mean, n - 1)
                run(project, n + 1, 2)
                run(variance, n - 1)
                run(scores, n, 1)
                run(project, n + 1, 3)
                run(weigh_values, n, 0)
                run(gate, n - 1)
                run(turn_probs, n, 1)
                run(project, n + 1, 4)

            for n in range(-1, 2):
                turn(n)
            with pe.Fori(2, STEPS - 1) as n:
                turn(n)
            for n in range(STEPS - 1, STEPS + 2):
                turn(n)

            pe.wait_ge(fin_done, 1)
            for i in range(BATCH * TILES):
                mm = nc.tensor.transpose(pe_lo[0][:, P * i:P * i + P], x2T[:, P * i:P * i + P], ident[:])
            mm.then_inc(fin_mm, 1)

        @block.scalar
        def _(act):
            act.wait_ge(loaded, 16 * n_loads)
            nc.scalar.activation(tgate[:], gates[:], ACT.Tanh).then_inc(pre_act, 1)

            def norm_part(k):
                act.wait_ge(pre_dve, k)
                nc.scalar.activation(sq_big, xn_big, ACT.Square).then_inc(pre_act, 1)

            act.wait_ge(qkv_all_mm, 1)
            nc.scalar.activation(k_all, pe_lo[1][:], ACT.Identity, bias=bk).then_inc(qkv_all_out, 1)
            norm_part(DVE_C1)
            act.wait_ge(qkv_all_mm, 2)
            nc.scalar.copy(v_tok[:, 1, :], pe_lo[0][:]).then_inc(qkv_all_out, 1)
            act.wait_ge(pre_pe, 4)
            act.wait_ge(pre_pool, POOL_CONST)
            nc.scalar.activation(sd_big, pe_hi[1][:], ACT.Sqrt, bias=eps[:, 0:1]).then_inc(pre_act, 1)

            act.wait_ge(qkv_all_mm, 3)
            nc.scalar.activation(q_all, pe_hi[0][:], ACT.Identity, bias=bq).then_inc(qkv_all_out, 1)

            with act.Fori(0, BATCH) as b:
                def copy_turned(h):
                    wait(act, xt_mm, b, h + 1)
                    if h >= 2:
                        wait(act, xo_mm, b, h - 1)
                    nc.scalar.copy(pT_x[:, h % 2], bank(4 + h % 2).rearrange("p (k q) -> p k q", k=TILES))\
                        .then_inc(xt_out.sem, 1)

                for h in range(XHEADS + 2):
                    if h < XHEADS:
                        wait(act, x_neg, b, h + 1)
                        if h >= 4:
                            wait(act, xt_mm, b, h - 3)
                        for t in range(TILES):
                            nc.scalar.activation(p_x[:, h % 4, t, :], bank(h % 4)[:, SEQ * t:SEQ * t + SEQ], ACT.Exp,
                                                 bias=xneg[:, h % 4, t:t + 1], scale=float(XDIM) ** -0.5)\
                                .then_inc(x_exp.sem, 1)
                    if h >= 2:
                        copy_turned(h - 2)

            norm_part(DVE_C2)
            act.wait_ge(pre_pe, 6)
            nc.scalar.activation(sd_big, pe_hi[1][:], ACT.Sqrt, bias=eps[:, 0:1]).then_inc(pre_act, 1)

            def take_qk(n, i):
                t, part = FILLS[i]
                wait(act, qkv_mm, n, i + 1)
                if later(n):
                    wait(act, qkT_mm, n - 1, 2 * t + 2)
                nc.scalar.copy(raw[:, t, INNER * part:INNER * part + INNER], FILL[:]).then_inc(qkv_copied.sem, 1)

            def square_qk(n, i):
                t, part = FILLS[i]
                wait(act, qkv_mm, n, i + 1)
                if t:
                    wait(act, norm2_done, n, 1)
                elif later(n):
                    wait(act, norm2_done, n - 1)
                nc.scalar.activation(squares[:, INNER * part:INNER * part + INNER], FILL[:], ACT.Square)\
                    .then_inc(squared.sem, 1)

            def take_v(n, i):
                wait(act, qkv_mm, n, i + 1)
                if later(n):
                    wait(act, v_moved, n - 1)
                nc.scalar.copy(v_tok[:, FILLS[i][0], :], FILL[:]).then_inc(qkv_copied.sem, 1)

            def root(n, t):
                wait(act, norm2_done, n, t + 1)
                nc.scalar.activation(norm[:, t, :], norm2[:, t, :], ACT.Sqrt).then_inc(norm_done.sem, 1)

            def copy_qkT(n, t, part):
                wait(act, qkT_mm, n, 2 * t + part + 1)
                nc.scalar.copy(qkT[:, PAIRS * part:PAIRS * part + PAIRS, P * t:P * t + P],
                               pe_lo[t][:].rearrange("p (a s) -> p a s", a=PAIRS)).then_inc(qkT_out.sem, 1)

            def exponent(n, t):
                wait(act, shifted, n, t + 1)
                nc.scalar.activation(probs[:, t, :], probs[:, t, :], ACT.Exp, scale=QK_SCALE).then_inc(exp_done.sem, 1)

            def copy_probsT(n, t):
                wait(act, pT_mm, n, t + 1)
                nc.scalar.copy(probsT[:, t, :], pe_lo[t][:]).then_inc(pT_out.sem, 1)

            def copy_attT(n, half):
                wait(act, attT_mm, n, half + 1)
                nc.scalar.copy(attT[:, 4 * half:4 * half + 4, :],
                               pe_hi[1][:].rearrange("p (a s) -> p a s", a=4)).then_inc(attT_out.sem, 1)

            def square_centred(n):
                wait(act, centre_done, n)
                nc.scalar.activation(centred2[:], centred[:], ACT.Square).then_inc(csq_done.sem, 1)

            def deviation(n):
                wait(act, var_mm, n)
                nc.scalar.activation(std[:], bank(6)[:, 0:SEQ], ACT.Sqrt, bias=eps[:, 0:1]).then_inc(std_done.sem, 1)

            def gates_of(n):
                for j, (f0, fs) in enumerate(CHUNKS):
                    wait(act, gate_mm, n, max(j, 1))
                    src = bank(7)[0:fs, SEQ * j:SEQ * j + SEQ] if j < 2 else bank(6)[0:fs, 0:SEQ]
                    nc.scalar.activation(gelu[0:fs, j, :], src, ACT.Gelu, bias=b_1[0:fs, 1, j:j + 1])\
                        .then_inc(gelu_done.sem, 1)

            def turn(n):
                nc.scalar.preload_act_table(ACT.Exp)
                run(exponent, n - 1, 0)
                run(copy_qkT, n - 1, 1, 0)
                run(take_qk, n, 1)
                run(copy_qkT, n - 1, 1, 1)
                run(square_centred, n - 2)
                nc.scalar.preload_act_table(ACT.Sqrt)
                run(root, n, 0)
                run(deviation, n - 2)
                run(take_qk, n, 2)
                run(square_qk, n, 2)
                run(copy_probsT, n - 1, 0)
                run(take_qk, n, 3)
                nc.scalar.preload_act_table(ACT.Exp)
                run(exponent, n - 1, 1)
                run(square_qk, n, 3)
                nc.scalar.preload_act_table(ACT.Gelu)
                run(gates_of, n - 2)
                run(take_v, n, 4)
                run(copy_probsT, n - 1, 1)
                run(take_v, n, 5)
                run(copy_qkT, n, 0, 0)
                nc.scalar.preload_act_table(ACT.Sqrt)
                run(root, n, 1)
                run(copy_qkT, n, 0, 1)
                run(take_qk, n + 1, 0)
                run(square_qk, n + 1, 0)
                run(copy_attT, n - 1, 0)
                run(copy_attT, n - 1, 1)
                run(square_qk, n + 1, 1)

            for n in range(-1, 2):
                turn(n)
            with act.Fori(2, STEPS - 1) as n:
                turn(n)
            for n in range(STEPS - 1, STEPS + 2):
                turn(n)

            act.wait_ge(fin_mm, 1)
            nc.scalar.copy(x_in[:], pe_lo[0][:].rearrange("p (a d) -> p a d", a=BATCH * TILES)).then_inc(fin_copied, 1)

        @block.vector
        def _(dve):
            done = [0]

            def link(ins):
                done[0] += 1
                ins.then_inc(pre_dve, 1)
                dve.wait_ge(pre_dve, done[0])

            dve.wait_ge(loaded, 16 * n_loads)
            link(nc.vector.tensor_copy(ident_bf[:], ident[:]))
            link(nc.vector.memset(xs[64:P, 0:1], 0.0))
            link(nc.vector.memset(xfT[64:P, 0:1], 0.0))
            for t in range(TILES):
                link(nc.vector.tensor_copy(window_mask[:, t], window_mask_f[:, t:t + 1, :].to_broadcast([P, 8, 64])))
            for buffer in (mask_top, ones_top):
                link(nc.vector.memset(buffer[:], 0.0))
            link(nc.vector.tensor_copy(mask_top[0:1, :], mask_u8[:]))
            link(nc.vector.tensor_scalar(mask_top[0:1, :], mask_top[0:1, :], -1e30 * float(XDIM) ** 0.5, None, ALU.mult))
            link(nc.vector.memset(ones_top[0:1, :], 1.0))
            dve.wait_ge(pre_pe, 1)
            link(nc.vector.tensor_copy(xT[:], pe_lo[0][:]))
            assert done[0] == DVE_XT
            dve.wait_ge(pre_pe, 2)
            link(nc.vector.tensor_copy(cT, pe_lo[1][:]))
            assert done[0] == DVE_CT

            def big_norm(src, dst, k, marks):
                dve.wait_ge(pre_pe, k)
                link(nc.vector.tensor_tensor(xn_big, src, pe_hi[0][:], ALU.subtract))
                assert done[0] == marks[0]
                dve.wait_ge(pre_act, marks[1])
                link(nc.vector.reciprocal(rs_big, sd_big))
                ins = nc.vector.tensor_tensor(dst, xn_big, rs_big, ALU.mult)
                return ins

            link(big_norm(xT[:], xnT, 3, (DVE_C1, 3)))
            assert done[0] == DVE_LN1

            with dve.Fori(0, BATCH) as b:
                bs = bass.ds(b * SEQ, SEQ)
                nc.vector.tensor_tensor(
                    v_aug[:, :, :, 0:XDIM], v_all[:, bass.ds(b * TILES, TILES)],
                    bv_row[:].rearrange("p (o h d) -> p o h d", o=1, d=XDIM).to_broadcast([P, TILES, XHEADS, XDIM]),
                    ALU.add).then_inc(xv_out.sem, 1)

                def maxima(h):
                    wait(dve, xs_mm, b, h + 1)
                    if h >= 4:
                        wait(dve, x_exp, b, 2 * (h - 3))
                    nc.vector.tensor_reduce(xmax[:, h % 4, :], bank(h % 4).rearrange("p (t k) -> p t k", t=TILES),
                                            AX.X, ALU.max).then_inc(x_max.sem, 1)
                    wait(dve, x_max, b, h + 1)
                    nc.vector.tensor_scalar(xneg[:, h % 4, :], xmax[:, h % 4, :], -float(XDIM) ** -0.5, None, ALU.mult)\
                        .then_inc(x_neg.sem, 1)

                def outputs(m):
                    wait(dve, xo_mm, b, PER * (m + 1))
                    if m:
                        wait(dve, xon_done, b, m)
                    nc.vector.tensor_copy(xo[:], bank(6 + m % 2)[:, 0:SEQ]).then_inc(xo_out.sem, 1)
                    wait(dve, xsum_mm, b, m + 1)
                    nc.vector.reciprocal(xrec[:], bank(6 + m % 2)[:, SEQ:2 * SEQ]).then_inc(xrec_done.sem, 1)
                    wait(dve, xrec_done, b, m + 1)
                    nc.vector.tensor_tensor(xon[:, m, :], xo[:], xrec[:], ALU.mult).then_inc(xon_done.sem, 1)

                for h in range(XHEADS + 4):
                    if h < XHEADS:
                        maxima(h)
                    if h >= 7 and (h - 7) % PER == 0:
                        outputs((h - 7) // PER)
                wait(dve, xy_mm, b)
                nc.vector.tensor_scalar(xtmp[:], bank(4)[:, 0:SEQ], bxo[:, 0:1], tgate[:, 0:1], ALU.add, ALU.mult)\
                    .then_inc(xy_scaled.sem, 1)
                wait(dve, xy_scaled, b)
                nc.vector.tensor_tensor(x2T[:, bs], xtmp[:], xT[:, bs], ALU.add).then_inc(xy_done.sem, 1)

            dve.wait_ge(xy_done.sem, BATCH)
            big_norm(x2T[:], xT[:], 5, (DVE_C2, 5)).then_inc(x_ready.sem, 1)

            def lengths(n, t):
                wait(dve, squared, n, 2 * t + 2)
                nc.vector.tensor_reduce(norm2[:, t, :], squares[:].rearrange("p (h d) -> p h d", d=HDIM), AX.X, ALU.add)\
                    .then_inc(norm2_done.sem, 1)

            def inverses(n, t):
                wait(dve, norm_done, n, t + 1)
                nc.vector.tensor_scalar(norm_c[:, t, :], norm[:, t, :], 1e-12, None, ALU.max).then_inc(normc_done.sem, 1)
                wait(dve, normc_done, n, t + 1)
                nc.vector.reciprocal(inv_norm[:, t, :], norm_c[:, t, :]).then_inc(inv_done.sem, 1)

            def sines(n, t):
                layer = n // BATCH
                wait(dve, qkv_copied, n, 2 * t + 2)
                if t:
                    wait(dve, qk_done, n, 1)
                elif later(n):
                    wait(dve, qk_done, n - 1)
                sine_half(nc.vector, n, t, 1).then_inc(sin_done.sem, 1)

            def rotate(n, t):
                wait(dve, sin_done, n, t + 1)
                wait(dve, swung, n, t + 1)
                wait(dve, cos_done, n, t + 1)
                nc.vector.tensor_tensor(by_sin[:], by_sin[:], by_cos[:], ALU.add).then_inc(rot_done.sem, 1)
                wait(dve, rot_done, n, t + 1)
                wait(dve, inv_done, n, t + 1)
                nc.vector.tensor_tensor(
                    raw[:, t, :].rearrange("p (h d) -> p h d", d=HDIM), by_sin[:].rearrange("p (h d) -> p h d", d=HDIM),
                    inv_norm[:, t, :].rearrange("p (h o) -> p h o", o=1).to_broadcast([P, 2 * HEADS, HDIM]), ALU.mult)\
                    .then_inc(qk_done.sem, 1)

            def heads_split(ap):
                return ap.rearrange("p (a o d) -> p o a d", o=2, d=64)

            def shift(n, t):
                wait(dve, s_mm, n, t + 1)
                ps = pe_lo[t][:].rearrange("p (o a d) -> p o a d", o=2, d=64)
                nc.vector.tensor_reduce(row_max[:, t, :], pe_lo[t][:].rearrange("p (h d) -> p h d", d=64), AX.X, ALU.max)\
                    .then_inc(max_done.sem, 1)
                wait(dve, max_done, n, t + 1)
                nc.vector.tensor_tensor(
                    heads_split(probs[:, t, :]), ps,
                    row_max[:, t, :].rearrange("p (o a d) -> p o a d", o=2, d=1).to_broadcast([P, 2, PAIRS, 64]),
                    ALU.subtract).then_inc(shifted.sem, 1)

            def sums(n, t):
                wait(dve, exp_done, n, t + 1)
                nc.vector.tensor_reduce(row_sum[:, t, :], probs[:, t, :].rearrange("p (h d) -> p h d", d=64), AX.X, ALU.add)\
                    .then_inc(sum_done.sem, 1)
                wait(dve, sum_done, n, t + 1)
                nc.vector.reciprocal(row_inv[:, t, :], row_sum[:, t, :]).then_inc(rinv_done.sem, 1)

            def take_att(n, t):
                wait(dve, pv_mm, n, t + 1)
                wait(dve, rinv_done, n, t + 1)
                nc.vector.tensor_tensor(
                    heads_split(att[:, t, :]), pe_lo[t][:].rearrange("p (o a d) -> p o a d", o=2, d=64),
                    row_inv[:, t, :].rearrange("p (a o d) -> p o a d", o=2, d=1).to_broadcast([P, 2, PAIRS, 64]),
                    ALU.mult).then_inc(att_done.sem, 1)

            def add_x(n):
                x0 = (n % BATCH) * SEQ
                wait(dve, y_mm, n)
                nc.vector.tensor_tensor(xfT[0:64, :], xT[0:64, bass.ds(x0, SEQ)], bank(6)[0:64, 0:SEQ], ALU.add)\
                    .then_inc(x1_done.sem, 1)
                nc.vector.tensor_tensor(xfT[64:P, 1:SEQ], xT[64:P, bass.ds(x0, SEQ - 1)], bank(6)[64:P, 0:SEQ - 1], ALU.add)\
                    .then_inc(x1_done.sem, 1)
                nc.vector.tensor_tensor(x1T[:], xT[:, bass.ds(x0, SEQ)], bank(6)[:, 0:SEQ], ALU.add)\
                    .then_inc(x1_done.sem, 1)

            def centre(n):
                wait(dve, mean_mm, n)
                wait(dve, x1_done, n)
                nc.vector.tensor_tensor(centred[:], xfT[:], bank(7)[:, 0:SEQ], ALU.subtract).then_inc(centre_done.sem, 1)

            def scale_norm(n):
                wait(dve, std_done, n)
                nc.vector.reciprocal(rstd[:], std[:]).then_inc(rstd_done.sem, 1)
                wait(dve, centre_done, n)
                wait(dve, rstd_done, n)
                nc.vector.tensor_tensor(normed[:], centred[:], rstd[:], ALU.mult).then_inc(normed_done.sem, 1)
                wait(dve, normed_done, n)
                dve.wait_ge(small_loaded, (n // BATCH + 1) * (16 * SMALLS))
                nc.vector.tensor_scalar(ffn_in[:], normed[:], ln_gb[:, 0:1], ln_gb[:, 1:2], ALU.mult, ALU.add)\
                    .then_inc(ffnin_done.sem, 1)

            def inner(n):
                wait(dve, up_mm, n)
                for j, (f0, fs) in enumerate(CHUNKS):
                    src = bank(7)[0:fs, SEQ * j:SEQ * j + SEQ] if j < 2 else bank(6)[0:fs, 0:SEQ]
                    nc.vector.scalar_tensor_tensor(hidden[0:fs, j, :], src, b_1[0:fs, 0, j:j + 1], gelu[0:fs, j, :],
                                                   ALU.add, ALU.mult).then_inc(hid_done.sem, 1)

            def new_x(n):
                x0 = (n % BATCH) * SEQ
                wait(dve, down_mm, n)
                nc.vector.scalar_tensor_tensor(xT[:, bass.ds(x0, SEQ)], bank(7)[:, 0:SEQ], b_2[:, 0:1], x1T[:],
                                               ALU.add, ALU.add).then_inc(x_ready.sem, 1)

            def turn(n):
                run(inverses, n, 1)
                run(take_att, n - 1, 1)
                run(new_x, n - 2)
                run(rotate, n, 1)
                run(shift, n, 0)
                run(lengths, n + 1, 0)
                run(sums, n, 0)
                run(add_x, n - 1)
                run(centre, n - 1)
                run(sines, n + 1, 0)
                run(scale_norm, n - 1)
                run(inverses, n + 1, 0)
                run(shift, n, 1)
                run(rotate, n + 1, 0)
                run(take_att, n, 0)
                run(lengths, n + 1, 1)
                run(inner, n - 1)
                run(sums, n, 1)
                run(sines, n + 1, 1)

            dve.wait_ge(pre_pool, POOL_ALL)
            for n in range(-1, 2):
                turn(n)
            with dve.Fori(2, STEPS - 1) as n:
                turn(n)
            for n in range(STEPS - 1, STEPS + 2):
                turn(n)

            wait(dve, x_ready, STEPS - 1)
            nc.vector.scalar_tensor_tensor(x2T[:], xT[:], tgate[:, 1:2], x2T[:], ALU.mult, ALU.add).then_inc(fin_done, 1)


def _laid_out(i):
    import numpy as np

    f32 = np.float32

    def by_group(a, axis):
        shape = a.shape[:axis] + (XHEADS, GROUP) + a.shape[axis + 1:]
        spread = np.zeros(shape, f32)
        at = (slice(None),) * axis + (slice(None), slice(0, XDIM))
        spread[at] = a.reshape(a.shape[:axis] + (XHEADS, XDIM) + a.shape[axis + 1:])
        return spread

    def by_chunk(a):
        padded = np.zeros(a.shape[:1] + (len(CHUNKS) * P,) + a.shape[2:], f32)
        padded[:, 0:FFN] = a
        return padded

    xcolumns = np.stack([i["L0_xattn_bq"], i["L0_xattn_bk"], i["L0_xattn_bo"]], 1)
    b1 = i["L0_ffn_b1"]
    columns = np.concatenate([by_chunk(b1[:, 0:FFN]).reshape(DEPTH, len(CHUNKS), P),
                              by_chunk(b1[:, FFN:]).reshape(DEPTH, len(CHUNKS), P),
                              i["L0_ffn_ln_g"].reshape(DEPTH, 1, P), i["L0_ffn_ln_b"].reshape(DEPTH, 1, P),
                              i["L0_ffn_b2"].reshape(DEPTH, 1, P)], 1).transpose(0, 2, 1)
    return {
        "x": i["x"], "ctx": i["ctx_1024"], "mask": i["mask_BxS2_bf0"],
        "g_xattn": i["g_xattn"], "g_ffn": i["g_ffn"],
        "Wq": i["L0_xattn_Wq"], "Wk": i["L0_xattn_Wk"], "Wv": i["L0_xattn_Wv"],
        "Wxo": by_group(i["L0_xattn_Wo"], 0).reshape(MGROUPS, P, DIM).transpose(1, 0, 2),
        "bv": i["L0_xattn_bv"], "xcolumns": xcolumns,
        "Wqkv": i["L0_ffn_Wqkv"], "q_scale": i["L0_ffn_q_scale"], "k_scale": i["L0_ffn_k_scale"],
        "Wo": i["L0_ffn_Wo"], "W1": i["L0_ffn_W1"], "W2": by_chunk(i["L0_ffn_W2"]), "columns": columns,
    }


def _shape_tables():
    import numpy as np

    f32 = np.float32
    half = np.arange(0, HDIM, 2, dtype=f32)
    t = np.arange(SEQ, dtype=f32)
    freqs = t[:, None] * (f32(1.0) / f32(10000.0) ** (half / f32(HDIM)))[None, :]
    scale = ((half + f32(0.4 * HDIM)) / f32(1.4 * HDIM))[None, :] ** ((t - SEQ // 2) / f32(WIN // 2))[:, None]
    two = lambda a: np.concatenate([a, a], -1)
    cos, sin, scale = two(np.cos(freqs)), np.concatenate([-np.sin(freqs), np.sin(freqs)], -1), two(scale)
    a, j = np.arange(WIN)[:, None], np.arange(2 * WIN)[None, :]
    seen = np.where(j < WIN, j >= a, j - WIN <= a)
    hidden = np.tile(np.where(seen, 0.0, -1e30), (WINDOWS, 1))
    hidden[:WIN, :WIN] = -1e30
    p = np.arange(P)
    ones_row = (p % GROUP == XDIM).astype(f32)
    return {
        "t_cos": np.concatenate([cos * scale, cos / scale], -1).astype(f32),
        "t_sin": np.concatenate([sin * scale, sin / scale], -1).astype(f32),
        "t_mask": hidden.astype(f32),
        "t_ident": np.eye(P, dtype=f32),
        "t_spread": ((p[:, None] // GROUP == p[None, :] // GROUP) * ones_row[:, None]).astype(f32),
        "t_headrows": (p[:, None] // XDIM == np.arange(XHEADS)[None, :]).astype(f32),
    }


def kernel(**inputs):
    import numpy as _np
    import concourse.bacc as _bacc
    from concourse import mybir as _mybir
    from concourse.bass_utils import run_bass_kernel_spmd as _run

    nc = _bacc.Bacc("TRN2", target_bir_lowering=False, num_devices=1)
    arrays, args = {}, []
    given = _laid_out({name: _np.asarray(a) for name, a in inputs.items()}) | _shape_tables()
    for name, a in given.items():
        arrays[f"in_{name}_dram"] = a = _np.ascontiguousarray(a)
        args.append(nc.dram_tensor(f"in_{name}_dram", a.shape, _mybir.dt.from_np(a.dtype), kind="ExternalInput").ap())
    out = nc.dram_tensor("out_0_dram", (BATCH, SEQ, DIM), _mybir.dt.float32, kind="ExternalOutput").ap()
    build(nc, *args, out)
    r = _run(nc, [arrays], core_ids=[0])
    return r.results[0]["out_0_dram"]
```

```python
from contextlib import ExitStack

import concourse.bass as bass
from concourse import mybir

ALU = mybir.AluOpType
ACT = mybir.ActivationFunctionType
AX = mybir.AxisListType
F32 = mybir.dt.float32
F32R = mybir.dt.float32r
BF16 = mybir.dt.bfloat16
U8 = mybir.dt.uint8

P = 128
BATCH, SEQ, DIM = 4, 256, 128
TILES = SEQ // P
TOKENS = BATCH * SEQ
XHEADS = 16
XDIM = DIM // XHEADS
GROUP = 32
PER = P // GROUP
MGROUPS = XHEADS // PER
DEPTH = 6
HEADS, HDIM, WIN = 16, 64, 32
INNER = HEADS * HDIM
PAIRS = HEADS // 2
QUADS = P // WIN
WINDOWS = SEQ // WIN
STEPS = DEPTH * BATCH
QK_SCALE = 8.0
FFN = DIM * 4 * 2 // 3
CHUNKS = [(0, 128), (128, 128), (256, FFN - 256)]
V_MOVES = 4 * QUADS
LCOLS = 2 * len(CHUNKS) + 3


class Signal:

    def __init__(self, sem, per=1, before=0):
        self.sem, self.per, self.before = sem, per, before

    def upto(self, n, k=None):
        return n * self.per + (self.before + (self.per if k is None else k))


def build(nc, x, ctx, mask, g_xattn, g_ffn, Wq, Wk, Wv, Wxo, bv, xcolumns,
          Wqkv, q_scale, k_scale, Wo, W1, W2, columns,
          t_cos, t_sin, t_mask, t_ident, t_spread, t_headrows, out):
    DVE_CENTRED, DVE_NORMED, DVE_XT, DVE_CT, DVE_XNT, DVE_ALL = 3, 10, 11, 12, 13, 19
    POOL_CONST, POOL_ALL = 5, 15
    with ExitStack() as stack:
        def sb(name, shape, dt=F32):
            return stack.enter_context(nc.sbuf_tensor(name, shape, dt))

        def sem(name):
            return stack.enter_context(nc.semaphore(name))

        ident = sb("ident", [P, P])
        ident_bf = sb("ident_bf", [P, P], BF16)
        window_mask = sb("window_mask", [P, TILES, 8, 64], BF16)
        mean_of = sb("mean_of", [P, P])
        eps = sb("eps", [P, 1])
        head_rows = sb("head_rows", [P, XHEADS])
        x_in = sb("x_in", [P, BATCH * TILES, DIM])
        mask_u8 = sb("mask_u8", [1, TOKENS], U8)
        mask_top = sb("mask_top", [P, TOKENS], BF16)
        ones_top = sb("ones_top", [P, P], BF16)
        gates = sb("gates", [P, 2])
        tgate = sb("tgate", [P, 2])

        xT = sb("xT", [P, TOKENS])
        x2T = sb("x2T", [P, TOKENS])

        xcol = sb("xcol", [P, 3])
        bq, bk, bxo = xcol[:, 0:1], xcol[:, 1:2], xcol[:, 2:3]
        x_sum = sb("x_sum", [P, BATCH * TILES])
        x_mean = sb("x_mean", [P, BATCH * TILES])
        x_var = sb("x_var", [P, BATCH * TILES])
        x_std = sb("x_std", [P, BATCH * TILES])
        x_rstd = sb("x_rstd", [P, BATCH * TILES])
        xmax = sb("xmax", [P, 4, TILES])
        xneg = sb("xneg", [P, 4, TILES])

        w_in = sb("w_in", [P, 3 * INNER])
        w_hi = sb("w_hi", [P, 3 * INNER], F32R)
        w_lo = sb("w_lo", [P, 3 * INNER], F32R)
        no_add = sb("no_add", [P, 1])
        w_o = sb("w_o", [P, PAIRS, DIM])
        w_1 = sb("w_1", [P, 2 * FFN])
        w_2 = sb("w_2", [P, len(CHUNKS), DIM])
        lcol = sb("lcol", [P, LCOLS])
        b_1 = lcol[:, 0:6].rearrange("p (h c) -> p h c", h=2)
        ln_gb, b_2 = lcol[:, 6:8], lcol[:, 8:9]
        rot_cos = sb("rot_cos", [P, DEPTH * TILES, 2 * HDIM])
        rot_sin = sb("rot_sin", [P, DEPTH * TILES, 2 * HDIM])

        xs = sb("xs", [P, SEQ])
        xs_hi = sb("xs_hi", [P, SEQ], F32R)
        xs_lo = sb("xs_lo", [P, SEQ], F32R)
        raw = sb("raw", [P, TILES, 2 * INNER])
        squares = sb("squares", [P, 2 * INNER])
        by_cos = sb("by_cos", [P, 2 * INNER])
        by_sin = sb("by_sin", [P, 2 * INNER])
        norm2 = sb("norm2", [P, TILES, 2 * HEADS])
        norm = sb("norm", [P, TILES, 2 * HEADS])
        norm_c = sb("norm_c", [P, TILES, 2 * HEADS])
        inv_norm = sb("inv_norm", [P, TILES, 2 * HEADS])
        v_tok = sb("v_tok", [P, TILES, INNER])
        v_win = sb("v_win", [P, WINDOWS, INNER // 2])
        qkT = sb("qkT", [P, 2 * PAIRS, SEQ])

        row_max = sb("row_max", [P, TILES, HEADS])
        row_sum = sb("row_sum", [P, TILES, HEADS])
        row_inv = sb("row_inv", [P, TILES, HEADS])
        probs = sb("probs", [P, TILES, HEADS * 64])
        probsT = sb("probsT", [P, TILES, PAIRS * P])
        att = sb("att", [P, TILES, INNER])
        attT = sb("attT", [P, PAIRS, SEQ])
        x1T = sb("x1T", [P, SEQ])
        xfT = sb("xfT", [P, SEQ])
        centred = sb("centred", [P, SEQ])
        centred2 = sb("centred2", [P, SEQ])
        std = sb("std", [P, SEQ])
        rstd = sb("rstd", [P, SEQ])
        normed = sb("normed", [P, SEQ])
        ffn_in = sb("ffn_in", [P, SEQ])
        gelu = sb("gelu", [P, len(CHUNKS), SEQ])
        hidden = sb("hidden", [P, len(CHUNKS), SEQ])

        carved = [0]

        def carve(*dims):
            start, n = carved[0], 1
            for d in dims:
                n *= d
            carved[0] += n
            flat = v_win[:].rearrange("p w c -> p (w c)")[:, start:start + n]
            return flat if len(dims) == 1 else flat.rearrange("p (a b) -> p a b", b=dims[1])

        window_mask_f = carve(TILES, 64)
        cos_in, sin_in, scales = carve(TILES, 2 * HDIM), carve(TILES, 2 * HDIM), carve(DEPTH, 2 * HDIM)
        wv_in, bv_row, spread = carve(DIM), carve(DIM), carve(P)
        wxo_pad = carve(MGROUPS, DIM)
        q_here, xo, xrec, xtmp = carve(SEQ), carve(SEQ), carve(SEQ), carve(SEQ)
        c_in = att[:, 0, :].rearrange("p (a d) -> p a d", d=DIM)
        xon = att[:, 1, :].rearrange("p (m s) -> p m s", m=MGROUPS)
        wq, wk = attT[:, 0, 0:DIM], attT[:, 1, 0:DIM]
        v_aug = attT[:, 4:8, :].rearrange("p a s -> p (a s)").rearrange("p (t h g) -> p t h g", t=TILES, g=GROUP)
        x_centred, x_normed = (by_sin[:, TOKENS * i:TOKENS * i + TOKENS].rearrange("p (i d) -> p i d", d=DIM)
                               for i in range(2))
        x_squares = x_normed
        cT = squares[:, 0:TOKENS]
        xnT = squares[:, TOKENS:2 * TOKENS]
        q_all, k_all = raw[:, 0, 0:TOKENS], raw[:, 0, TOKENS:2 * TOKENS]
        v_all = v_tok[:, 1, :].rearrange("p (t h d) -> p t h d", h=XHEADS, d=XDIM)
        q_head = qkT
        p_x = raw[:, 1, :].rearrange("p (r q k) -> p r q k", r=4, q=TILES)
        pT_x = by_cos[:].rearrange("p (r k q) -> p r k q", r=4, k=TILES)

        pe_lo = [stack.enter_context(nc.psum_tensor(f"ps_s{i}", [P, 1024], F32)) for i in range(2)]
        pe_hi = [stack.enter_context(nc.psum_tensor(f"ps_g{i}", [P, 1024], F32)) for i in range(2)]

        FILLS = [(0, 0), (0, 1), (1, 0), (1, 1), (0, 2), (1, 2)]
        FILL = pe_hi[0]

        def bank(i):
            t = (pe_lo + pe_hi)[i // 2]
            return t[:, 512 * (i % 2):512 * (i % 2) + 512]

        x_loaded = sem("x_loaded")
        c_loaded = sem("c_loaded")
        loaded = sem("loaded")
        pre_dve = sem("pre_dve")
        pre_pool = sem("pre_pool")
        pre_act = sem("pre_act")
        pre_pe = sem("pre_pe")
        qkv_all_mm = sem("qkv_all_mm")
        qkv_all_out = sem("qkv_all_out")
        q_taken = Signal(sem("q_taken"))
        q_headed = Signal(sem("q_headed"), XHEADS)
        xv_out = Signal(sem("xv_out"))
        xs_mm = Signal(sem("xs_mm"), XHEADS)
        x_max = Signal(sem("x_max"), XHEADS)
        x_neg = Signal(sem("x_neg"), XHEADS)
        x_exp = Signal(sem("x_exp"), 2 * XHEADS)
        xt_mm = Signal(sem("xt_mm"), XHEADS)
        xt_out = Signal(sem("xt_out"), XHEADS)
        xo_mm = Signal(sem("xo_mm"), XHEADS)
        xo_out = Signal(sem("xo_out"), MGROUPS)
        xsum_mm = Signal(sem("xsum_mm"), MGROUPS)
        xrec_done = Signal(sem("xrec_done"), MGROUPS)
        xon_done = Signal(sem("xon_done"), MGROUPS)
        xy_mm = Signal(sem("xy_mm"))
        xy_scaled = Signal(sem("xy_scaled"))
        xy_done = Signal(sem("xy_done"))
        xmean_mm = Signal(sem("xmean_mm"))
        xcentred = Signal(sem("xcentred"))
        xsquared = Signal(sem("xsquared"))
        xvar_mm = Signal(sem("xvar_mm"))
        xdeviated = Signal(sem("xdeviated"))
        xinverted = Signal(sem("xinverted"))
        w_loaded = sem("w_loaded")
        w_split = Signal(sem("w_split"), 6)
        x_shifted = Signal(sem("x_shifted"), 2)
        out_loaded = sem("out_loaded")
        small_loaded = sem("small_loaded")
        x_ready = Signal(sem("x_ready"), 1, BATCH)
        xs_ready = Signal(sem("xs_ready"), 2)
        qkv_mm = Signal(sem("qkv_mm"), 6)
        qkv_copied = Signal(sem("qkv_copied"), 6)
        squared = Signal(sem("squared"), 4)
        norm2_done = Signal(sem("norm2_done"), 2)
        norm_done = Signal(sem("norm_done"), 2)
        normc_done = Signal(sem("normc_done"), 2)
        inv_done = Signal(sem("inv_done"), 2)
        cos_done = Signal(sem("cos_done"), 2)
        sin_done = Signal(sem("sin_done"), 2)
        swung = Signal(sem("swung"), 2)
        rot_done = Signal(sem("rot_done"), 2)
        qk_done = Signal(sem("qk_done"), 2)
        qkT_mm = Signal(sem("qkT_mm"), 4)
        qkT_out = Signal(sem("qkT_out"), 4)
        v_moved = Signal(sem("v_moved"), 16 * V_MOVES)
        s_mm = Signal(sem("s_mm"), 2)
        max_done = Signal(sem("max_done"), 2)
        shifted = Signal(sem("shifted"), 2)
        exp_done = Signal(sem("exp_done"), 2)
        sum_done = Signal(sem("sum_done"), 2)
        rinv_done = Signal(sem("rinv_done"), 2)
        pT_mm = Signal(sem("pT_mm"), 2)
        pT_out = Signal(sem("pT_out"), 2)
        pv_mm = Signal(sem("pv_mm"), 2)
        att_done = Signal(sem("att_done"), 2)
        attT_mm = Signal(sem("attT_mm"), 2)
        attT_out = Signal(sem("attT_out"), 2)
        y_mm = Signal(sem("y_mm"))
        x1_done = Signal(sem("x1_done"), 3)
        mean_mm = Signal(sem("mean_mm"))
        centre_done = Signal(sem("centre_done"))
        csq_done = Signal(sem("csq_done"))
        var_mm = Signal(sem("var_mm"))
        std_done = Signal(sem("std_done"))
        rstd_done = Signal(sem("rstd_done"))
        normed_done = Signal(sem("normed_done"))
        ffnin_done = Signal(sem("ffnin_done"))
        gate_mm = Signal(sem("gate_mm"), 2)
        up_mm = Signal(sem("up_mm"))
        gelu_done = Signal(sem("gelu_done"), 3)
        hid_done = Signal(sem("hid_done"), 3)
        down_mm = Signal(sem("down_mm"))
        fin_done = sem("fin_done")
        fin_mm = sem("fin_mm")
        fin_copied = sem("fin_copied")
        stored = sem("stored")

        def token_tiles(a):
            return a.rearrange("b (t p) d -> p (b t) d", p=P)

        def halves(ap, half):
            return ap.rearrange("p (k h d) -> p k h d", k=2, d=HDIM)[:, :, :, 32 * half:32 * half + 32]

        def sine_half(engine, n, t, half):
            table = rot_sin[:, bass.ds(n // BATCH * TILES + t, 1), :].rearrange("p o (k h d) -> p (o k) h d", k=2, h=1)
            return engine.tensor_tensor(
                halves(by_sin[:], half), halves(raw[:, t, :], 1 - half),
                table[:, :, :, 32 * half:32 * half + 32].to_broadcast([P, 2, HEADS, 32]), ALU.mult)

        loads = []

        def later(n):
            return not isinstance(n, int) or n > 0

        def run(stage, n, *args, steps=STEPS):
            if not isinstance(n, int) or 0 <= n < steps and (stage, n, args) not in ahead:
                stage(n, *args)

        ahead = []

        def run_ahead(b, h, stages):
            for at, stage, *args in stages:
                if isinstance(b, int) and b == BATCH and at == h:
                    stage(0, *args)
                    ahead.append((stage, 0, tuple(args)))

        HEAD_BANK = [h % 3 for h in range(XHEADS - 1)] + [3]
        LEND = 3

        def run_head(stage, b, h, back):
            run(stage, b if h >= back else b - 1, (h - back) % XHEADS, steps=BATCH)

        def run_group(stage, b, h, back):
            if (h - back) % PER == PER - 1:
                run(stage, b if h >= back else b - 1, (h - back) % XHEADS // PER, steps=BATCH)

        def wait_head(engine, signal, b, h, back=0, each=1):
            if h >= back:
                wait(engine, signal, b, each * (h - back + 1))
            elif later(b):
                wait(engine, signal, b - 1, each * (h - back + XHEADS + 1))

        def wait(engine, signal, n, k=None):
            engine.wait_ge(signal.sem, signal.upto(n, k))

        block = stack.enter_context(nc.Block())

        @block.sync
        def _(sp):
            def load(dst, src):
                loads.append(dst)
                sp.dma_start(dst, src).then_inc(loaded, 16)

            sp.dma_start(x_in[:], token_tiles(x)).then_inc(x_loaded, 16)
            sp.dma_start(ident[:], t_ident).then_inc(x_loaded, 16)
            sp.dma_start(c_in, token_tiles(ctx)).then_inc(c_loaded, 16)
            load(wq, Wq)
            load(wk, Wk)
            load(wxo_pad, Wxo)
            load(xcol[:], xcolumns)
            load(wv_in, Wv)
            load(mask_u8[:], mask.rearrange("(o b) s -> o (b s)", o=1))
            load(gates[:, 0:1], g_xattn.rearrange("(o d) -> o d", o=1).partition_broadcast(P))
            load(gates[:, 1:2], g_ffn.rearrange("(o d) -> o d", o=1).partition_broadcast(P))
            load(bv_row, bv.rearrange("(o d) -> o d", o=1).partition_broadcast(P))
            load(spread, t_spread)
            load(head_rows[:], t_headrows)
            load(cos_in, t_cos.rearrange("(t p) d -> p t d", p=P))
            load(sin_in, t_sin.rearrange("(t p) d -> p t d", p=P))
            load(window_mask_f, t_mask.rearrange("(t p) d -> p t d", p=P))
            load(scales[:, :, 0:HDIM], q_scale.rearrange("(o l) d -> o l d", o=1).partition_broadcast(P))
            load(scales[:, :, HDIM:], k_scale.rearrange("(o l) d -> o l d", o=1).partition_broadcast(P))

            def load_qkv(layer):
                sp.dma_start(w_in[:], Wqkv[layer]).then_inc(w_loaded, 16)

            def load_out(layer):
                sp.dma_start(w_o[:], Wo[layer].rearrange("(c p) d -> p c d", p=P)).then_inc(out_loaded, 16)

            def load_small(layer):
                sp.dma_start(w_1[:], W1[layer]).then_inc(small_loaded, 16)
                sp.dma_start(w_2[:], W2[layer].rearrange("(c p) d -> p c d", p=P)).then_inc(small_loaded, 16)
                sp.dma_start(lcol[:], columns[layer]).then_inc(small_loaded, 16)

            def move_values(n, first=False):
                wait(sp, qkv_copied, n)
                if not first:
                    wait(sp, pv_mm, n - 1)
                for odd in range(2):
                    cols = slice(512 * odd, 512 * odd + 512)
                    for c in range(QUADS):
                        src = v_tok[WIN * c:WIN * c + WIN, :, cols]
                        own = slice(64 * odd + 32, 64 * odd + 64)
                        before = slice(64 * odd, 64 * odd + 32)
                        sp.dma_start(v_win[own, c:WINDOWS:QUADS, :], src).then_inc(v_moved.sem, 16)
                        if c < QUADS - 1:
                            sp.dma_start(v_win[before, c + 1:WINDOWS:QUADS, :], src).then_inc(v_moved.sem, 16)
                        else:
                            sp.dma_start(v_win[before, QUADS, :], src[:, 0]).then_inc(v_moved.sem, 16)

            load_qkv(0)
            load_out(0)
            load_small(0)
            move_values(0, first=True)
            with sp.Fori(1, DEPTH) as layer:
                with sp.Fori(1, BATCH - 1) as j:
                    move_values(layer * BATCH + j - BATCH)
                wait(sp, w_split, layer - 1)
                load_qkv(layer)
                move_values(layer * BATCH - 1)
                move_values(layer * BATCH)
                wait(sp, y_mm, layer * BATCH - 1)
                load_out(layer)
                wait(sp, x_ready, layer * BATCH - 1)
                load_small(layer)
            with sp.Fori(STEPS - BATCH + 1, STEPS) as n:
                move_values(n)

            sp.wait_ge(fin_copied, 1)
            sp.dma_start(token_tiles(out), x_in[:]).then_inc(stored, 16)
            sp.wait_ge(stored, 16)

        n_loads = len(loads)
        SMALLS = 3

        @block.gpsimd
        def _(pool):
            nc.gpsimd.memset(eps[:], 1e-5).then_inc(pre_pool, 1)
            nc.gpsimd.memset(no_add[:], 0.0).then_inc(pre_pool, 1)
            nc.gpsimd.memset(mean_of[:], 1.0 / DIM).then_inc(pre_pool, 1)
            nc.gpsimd.memset(v_aug, 0.0).then_inc(pre_pool, 1)
            pool.wait_ge(pre_pool, 4)
            nc.gpsimd.memset(v_aug[:, :, :, XDIM:XDIM + 1], 1.0).then_inc(pre_pool, 1)
            pool.wait_ge(loaded, 16 * n_loads)
            for t in range(TILES):
                nc.gpsimd.tensor_tensor(rot_cos[:, t::TILES, :], cos_in[:, t:t + 1, :].to_broadcast([P, DEPTH, 2 * HDIM]),
                                        scales, ALU.mult).then_inc(pre_pool, 1)
                for qk in range(2):
                    for half in range(2):
                        d = HDIM * qk + 32 * half
                        o = HDIM * qk + 32 * (1 - half)
                        nc.gpsimd.tensor_tensor(rot_sin[:, t::TILES, d:d + 32],
                                                sin_in[:, t:t + 1, d:d + 32].to_broadcast([P, DEPTH, 32]),
                                                scales[:, :, o:o + 32], ALU.mult).then_inc(pre_pool, 1)

            def head_queries(b, first=False):
                if not first:
                    wait(pool, q_headed, b - 1)
                nc.gpsimd.tensor_copy(q_here, q_all[:, bass.ds(b * SEQ, SEQ)]).then_inc(q_taken.sem, 1)
                wait(pool, q_taken, b)
                for h in range(XHEADS):
                    if not first:
                        wait(pool, xs_mm, b - 1, h + 1)
                    nc.gpsimd.tensor_tensor(q_head[:, h, :], q_here, head_rows[:, h:h + 1].to_broadcast([P, SEQ]),
                                            ALU.mult).then_inc(q_headed.sem, 1)

            pool.wait_ge(qkv_all_out, 3)
            head_queries(0, first=True)
            with pool.Fori(1, BATCH) as b:
                head_queries(b)

            def split(columns, src, hi, lo, signal, n, k):
                nc.gpsimd.tensor_tensor(hi, src, no_add[:].to_broadcast([P, columns]), ALU.add).then_inc(signal.sem, 1)
                wait(pool, signal, n, k)
                nc.gpsimd.tensor_tensor(lo, src, hi.bitcast(F32), ALU.subtract).then_inc(signal.sem, 1)

            def split_weights(layer, part):
                cols = slice(INNER * part, INNER * part + INNER)
                pool.wait_ge(w_loaded, (layer + 1) * 16)
                if later(layer):
                    wait(pool, qkv_mm, layer * BATCH - 1, (3, 4, 6)[part])
                split(INNER, w_in[:, cols], w_hi[:, cols], w_lo[:, cols], w_split, layer, 2 * part + 1)

            def shift_x(n):
                wait(pool, x_ready, n - BATCH)
                if later(n):
                    wait(pool, xs_ready, n - 1)
                    wait(pool, cos_done, n - 1)
                    wait(pool, swung, n - 1)
                b = n % BATCH
                nc.gpsimd.tensor_tensor(xs[0:64, :], xT[0:64, bass.ds(b * SEQ, SEQ)],
                                        no_add[0:64, :].to_broadcast([64, SEQ]), ALU.add).then_inc(x_shifted.sem, 1)
                wait(pool, x_shifted, n, 1)
                nc.gpsimd.tensor_tensor(xs[64:P, 1:SEQ], xT[64:P, bass.ds(b * SEQ, SEQ - 1)],
                                        no_add[64:P, :].to_broadcast([64, SEQ - 1]), ALU.add).then_inc(x_shifted.sem, 1)
                wait(pool, x_shifted, n)
                if later(n):
                    wait(pool, qkv_mm, n - 1)
                split(SEQ, xs[:], xs_hi[:], xs_lo[:], xs_ready, n, 1)
                wait(pool, xs_ready, n)

            def cosines(n, t):
                layer = n // BATCH
                wait(pool, qkv_copied, n, 2 * t + 2)
                if t:
                    wait(pool, rot_done, n, 1)
                elif later(n):
                    wait(pool, rot_done, n - 1)
                nc.gpsimd.tensor_tensor(
                    by_cos[:].rearrange("p (k h d) -> p k h d", k=2, d=HDIM),
                    raw[:, t, :].rearrange("p (k h d) -> p k h d", k=2, d=HDIM),
                    rot_cos[:, bass.ds(layer * TILES + t, 1), :].rearrange("p o (k h d) -> p (o k) h d", k=2, h=1)
                    .to_broadcast([P, 2, HEADS, HDIM]), ALU.mult).then_inc(cos_done.sem, 1)

            def swing(n, t):
                if t:
                    wait(pool, qk_done, n, 1)
                elif later(n):
                    wait(pool, qk_done, n - 1)
                sine_half(nc.gpsimd, n, t, 0).then_inc(swung.sem, 1)

            def steps(layer):
                for b in range(BATCH):
                    n = layer * BATCH + b
                    shift_x(n)
                    if b == 0:
                        split_weights(layer, 1)
                        split_weights(layer, 2)
                    cosines(n, 0)
                    swing(n, 0)
                    if b == BATCH - 1:
                        run(split_weights, layer + 1, 0, steps=DEPTH)
                    cosines(n, 1)
                    swing(n, 1)

            split_weights(0, 0)
            steps(0)
            with pool.Fori(1, DEPTH - 1) as layer:
                steps(layer)
            steps(DEPTH - 1)

        @block.tensor
        def _(pe):
            def turn_all(src, out_ps):
                for i in range(BATCH * TILES):
                    mm = nc.tensor.transpose(out_ps[:, P * i:P * i + P], src[:, i, :], ident[:])
                mm.then_inc(pre_pe, 1)

            def project_all(w, src, out_ps):
                for j in range(2):
                    mm = nc.tensor.matmul(out_ps[:, 512 * j:512 * j + 512], w, src[:, 512 * j:512 * j + 512],
                                          start=True, stop=True)
                mm.then_inc(qkv_all_mm, 1)

            pe.wait_ge(x_loaded, 32)
            turn_all(x_in, pe_lo[0])
            pe.wait_ge(c_loaded, 16)
            turn_all(c_in, pe_lo[1])
            pe.wait_ge(pre_dve, DVE_NORMED)
            turn_all(x_normed, pe_hi[0])
            pe.wait_ge(loaded, 16 * n_loads)
            pe.wait_ge(pre_dve, DVE_CT)
            project_all(wk, cT, pe_lo[1])
            for i in range(BATCH * TILES):
                mm = nc.tensor.matmul(pe_lo[0][:, P * i:P * i + P], cT[:, P * i:P * i + P], wv_in, start=True, stop=True)
            mm.then_inc(qkv_all_mm, 1)
            pe.wait_ge(pre_dve, DVE_XNT)
            project_all(wq, xnT, pe_hi[1])

            pe.wait_ge(pre_dve, DVE_ALL)
            pe.wait_ge(pre_pool, POOL_CONST)
            pe.wait_ge(qkv_all_out, 3)

            def scores(b, h):
                wait(pe, q_headed, b, h + 1)
                if HEAD_BANK[h] != LEND:
                    wait_head(pe, x_exp, b, h, back=3 if h >= 3 else 4, each=2)
                elif later(b):
                    wait(pe, xdeviated, b - 1)
                for t in range(TILES):
                    o = bank(HEAD_BANK[h])[:, SEQ * t:SEQ * t + SEQ]
                    nc.tensor.matmul(o, ones_top[:], mask_top[:, bass.ds(b * SEQ, SEQ)], start=True, stop=False)
                    mm = nc.tensor.matmul(o, q_head[:, h, P * t:P * t + P], k_all[:, bass.ds(b * SEQ, SEQ)],
                                          start=False, stop=True)
                mm.then_inc(xs_mm.sem, 1)

            def turn(b, h):
                wait(pe, x_exp, b, 2 * (h + 1))
                wait_head(pe, xt_out, b, h, back=2)
                for k in range(TILES):
                    for t in range(TILES):
                        mm = nc.tensor.transpose(bank(4 + h % 2)[:, SEQ * k + P * t:SEQ * k + P * t + P],
                                                 p_x[:, h % 4, t, P * k:P * k + P], ident[:])
                mm.then_inc(xt_mm.sem, 1)

            def values(b, h):
                m, g = divmod(h, PER)
                wait(pe, xt_out, b, h + 1)
                if h == 0:
                    wait(pe, xv_out, b)
                if g == 0:
                    if m >= 2:
                        wait(pe, xrec_done, b, m - 1)
                    elif later(b):
                        wait(pe, xrec_done, b - 1, m + 3)
                for k in range(TILES):
                    mm = nc.tensor.matmul(bank(6 + m % 2)[GROUP * g:GROUP * g + GROUP, 0:SEQ], v_aug[:, k, h, :],
                                          pT_x[:, h % 4, k, :], start=(k == 0), stop=(k == 1),
                                          tile_position=(0, GROUP * g))
                mm.then_inc(xo_mm.sem, 1)

            def sums(b, m):
                wait(pe, xo_out, b, m + 1)
                nc.tensor.matmul(bank(6 + m % 2)[:, SEQ:2 * SEQ], spread, xo, start=True, stop=True)\
                    .then_inc(xsum_mm.sem, 1)

            def project_out(b):
                wait(pe, xon_done, b)
                wait(pe, x_exp, b)
                for m in range(MGROUPS):
                    mm = nc.tensor.matmul(bank(LEND)[:, 0:SEQ], wxo_pad[:, m, :], xon[:, m, :], start=(m == 0),
                                          stop=(m == MGROUPS - 1))
                mm.then_inc(xy_mm.sem, 1)

            def mean_out(b):
                wait(pe, xy_done, b)
                nc.tensor.matmul(bank(LEND)[:, 0:SEQ], mean_of[:], x2T[:, bass.ds(b * SEQ, SEQ)], start=True, stop=True)\
                    .then_inc(xmean_mm.sem, 1)

            def variance_out(b):
                wait(pe, xsquared, b)
                nc.tensor.matmul(bank(LEND)[:, 0:SEQ], mean_of[:], centred2[:], start=True, stop=True)\
                    .then_inc(xvar_mm.sem, 1)

            def project(n, i):
                t, part = FILLS[i]
                wait(pe, w_split, n // BATCH, 2 * part + 2)
                if i:
                    wait(pe, qkv_copied, n, i)
                    if i < 5:
                        wait(pe, squared, n, i)
                else:
                    wait(pe, xs_ready, n)
                    if later(n):
                        wait(pe, qkv_copied, n - 1)
                for j in range(2):
                    def cols(w):
                        if part < 2:
                            return w[:, INNER * part + 512 * j:INNER * part + 512 * j + 512]
                        return w[:, 2 * INNER:].rearrange("p (h o d) -> p o h d", o=2, d=HDIM)[:, j]

                    for k, (x_part, w) in enumerate([(xs_hi, w_hi), (xs_hi, w_lo), (xs_lo, w_hi)]):
                        mm = nc.tensor.matmul(FILL[:, 512 * j:512 * j + 512], x_part[:, P * t:P * t + P], cols(w),
                                              start=(k == 0), stop=(k == 2))
                mm.then_inc(qkv_mm.sem, 1)

            def heads(b):
                for h in range(XHEADS):
                    run(scores, b, h, steps=BATCH)
                    run_head(turn, b, h, 2)
                    run_head(values, b, h, 4)
                    run_group(sums, b, h, 5)
                    for at, stage in (7, project_out), (9, mean_out), (12, variance_out):
                        if h == at:
                            run(stage, b - 1, steps=BATCH)
                    run_ahead(b, h, [(5, project, 0), (8, project, 1), (10, project, 2), (12, project, 3)])

            heads(0)
            with pe.Fori(1, BATCH) as b:
                heads(b)
            heads(BATCH)

            def turn_qk(n, t, part):
                if part:
                    wait(pe, qkT_out, n, 2 * t + 1)
                else:
                    wait(pe, qk_done, n, t + 1)
                    if later(n):
                        wait(pe, att_done, n - 1, t + 1)
                for p in range(PAIRS):
                    mm = nc.tensor.transpose(pe_lo[t][:, P * p:P * p + P],
                                             raw[:, t, P * (PAIRS * part + p):P * (PAIRS * part + p) + P], ident[:])
                mm.then_inc(qkT_mm.sem, 1)

            def scores(n, t):
                wait(pe, qkT_out, n, 2 * t + 2)
                ps = pe_lo[t]
                for odd in range(2):
                    nc.tensor.matmul(ps[:, 512 * odd:512 * odd + 512], ident_bf[:], window_mask[:, t], start=True,
                                     stop=False, skip_group_check=True)
                for h in range(HEADS):
                    rows = slice(64 * (h % 2), 64 * (h % 2) + 64)
                    for c in range(QUADS):
                        w = QUADS * t + c
                        k0 = WIN * max(w - 1, 0)
                        keys = WIN * (w + 1) - k0
                        o = 512 * (h % 2) + 64 * (h // 2) + 64 - keys
                        mm = nc.tensor.matmul(ps[WIN * c:WIN * c + WIN, o:o + keys],
                                              qkT[rows, h // 2, WIN * w:WIN * w + WIN],
                                              qkT[rows, PAIRS + h // 2, k0:k0 + keys],
                                              start=False, stop=True, skip_group_check=True,
                                              tile_position=(64 * (h % 2), WIN * c))
                mm.then_inc(s_mm.sem, 1)

            def turn_probs(n, t):
                wait(pe, exp_done, n, t + 1)
                for p in range(PAIRS):
                    mm = nc.tensor.transpose(pe_lo[t][:, P * p:P * p + P], probs[:, t, P * p:P * p + P], ident[:])
                mm.then_inc(pT_mm.sem, 1)

            def weigh_values(n, t):
                wait(pe, pT_out, n, t + 1)
                wait(pe, v_moved, n)
                nc.tensor.matmul(pe_lo[t][:, 0:2], ident_bf[:], ident_bf[:, 0:2], start=True, stop=True)
                for h in range(HEADS):
                    odd = h % 2
                    for c in range(QUADS):
                        w = QUADS * t + c
                        r0 = 64 * odd + (32 if w == 0 else 0)
                        rows = slice(r0, 64 * odd + 64)
                        o = 512 * odd + 64 * (h // 2)
                        mm = nc.tensor.matmul(pe_lo[t][WIN * c:WIN * c + WIN, o:o + 64],
                                              probsT[rows, t, P * (h // 2) + WIN * c:P * (h // 2) + WIN * c + WIN],
                                              v_win[rows, w, 64 * (h // 2):64 * (h // 2) + 64],
                                              start=True, stop=True, skip_group_check=True,
                                              tile_position=(r0, WIN * c))
                mm.then_inc(pv_mm.sem, 1)

            def turn_att(n, half):
                if half:
                    wait(pe, attT_out, n, 1)
                else:
                    wait(pe, att_done, n)
                    wait(pe, x_ready, n - 1)
                for p in range(4):
                    for t in range(TILES):
                        mm = nc.tensor.transpose(pe_hi[1][:, SEQ * p + P * t:SEQ * p + P * t + P],
                                                 att[:, t, P * (4 * half + p):P * (4 * half + p) + P], ident[:])
                mm.then_inc(attT_mm.sem, 1)

            def out_project(n):
                wait(pe, attT_out, n)
                pe.wait_ge(out_loaded, (n // BATCH + 1) * 16)
                for p in range(PAIRS):
                    mm = nc.tensor.matmul(bank(6)[:, 0:SEQ], w_o[:, p, :], attT[:, p, :], start=(p == 0),
                                          stop=(p == PAIRS - 1))
                mm.then_inc(y_mm.sem, 1)

            def mean(n):
                wait(pe, x1_done, n)
                nc.tensor.matmul(bank(7)[:, 0:SEQ], mean_of[:], xfT[:], start=True, stop=True).then_inc(mean_mm.sem, 1)

            def variance(n):
                wait(pe, csq_done, n)
                nc.tensor.matmul(bank(6)[:, 0:SEQ], mean_of[:], centred2[:], start=True, stop=True).then_inc(var_mm.sem, 1)

            def ffn_bank(j, rows):
                return bank(7)[0:rows, SEQ * j:SEQ * j + SEQ] if j < 2 else bank(6)[0:rows, 0:SEQ]

            def gate(n):
                wait(pe, ffnin_done, n)
                pe.wait_ge(small_loaded, (n // BATCH + 1) * (16 * SMALLS))
                for j, (f0, fs) in enumerate(CHUNKS):
                    mm = nc.tensor.matmul(ffn_bank(j, fs), w_1[:, FFN + f0:FFN + f0 + fs], ffn_in[:],
                                          start=True, stop=True)
                    if j:
                        mm.then_inc(gate_mm.sem, 1)

            def up(n):
                for j, (f0, fs) in enumerate(CHUNKS):
                    wait(pe, gelu_done, n, max(j + 1, 2))
                    mm = nc.tensor.matmul(ffn_bank(j, fs), w_1[:, f0:f0 + fs], ffn_in[:], start=True, stop=True)
                mm.then_inc(up_mm.sem, 1)

            def down(n):
                wait(pe, hid_done, n)
                for j, (f0, fs) in enumerate(CHUNKS):
                    mm = nc.tensor.matmul(bank(7)[:, 0:SEQ], w_2[0:fs, j, :], hidden[0:fs, j, :], start=(j == 0),
                                          stop=(j == 2))
                mm.then_inc(down_mm.sem, 1)

            def turn(n):
                run(up, n - 2)
                run(turn_qk, n, 0, 0)
                run(project, n, 5)
                run(weigh_values, n - 1, 1)
                run(down, n - 2)
                run(turn_qk, n, 0, 1)
                run(project, n + 1, 0)
                run(turn_att, n - 1, 0)
                run(scores, n, 0)
                run(turn_att, n - 1, 1)
                run(project, n + 1, 1)
                run(turn_qk, n, 1, 0)
                run(out_project, n - 1)
                run(turn_probs, n, 0)
                run(turn_qk, n, 1, 1)
                run(mean, n - 1)
                run(project, n + 1, 2)
                run(variance, n - 1)
                run(scores, n, 1)
                run(project, n + 1, 3)
                run(weigh_values, n, 0)
                run(gate, n - 1)
                run(turn_probs, n, 1)
                run(project, n + 1, 4)

            for n in range(-1, 2):
                turn(n)
            with pe.Fori(2, STEPS - 1) as n:
                turn(n)
            for n in range(STEPS - 1, STEPS + 2):
                turn(n)

            pe.wait_ge(fin_done, 1)
            for i in range(BATCH * TILES):
                mm = nc.tensor.transpose(pe_lo[0][:, P * i:P * i + P], x2T[:, P * i:P * i + P], ident[:])
            mm.then_inc(fin_mm, 1)

        @block.scalar
        def _(act):
            nc.scalar.preload_act_table(ACT.Sqrt)
            act.wait_ge(pre_dve, DVE_CENTRED)
            nc.scalar.activation(x_squares, x_centred, ACT.Square).then_inc(pre_act, 1)
            act.wait_ge(pre_dve, DVE_NORMED - 2)
            act.wait_ge(pre_pool, 1)
            nc.scalar.activation(x_std[:], x_var[:], ACT.Sqrt, bias=eps[:, 0:1], scale=1.0 / DIM).then_inc(pre_act, 1)
            act.wait_ge(loaded, 16 * n_loads)
            nc.scalar.activation(tgate[:], gates[:], ACT.Tanh).then_inc(pre_act, 1)
            nc.scalar.preload_act_table(ACT.Exp)
            act.wait_ge(qkv_all_mm, 1)
            nc.scalar.activation(k_all, pe_lo[1][:], ACT.Identity, bias=bk).then_inc(qkv_all_out, 1)
            act.wait_ge(qkv_all_mm, 2)
            nc.scalar.copy(v_tok[:, 1, :], pe_lo[0][:]).then_inc(qkv_all_out, 1)
            act.wait_ge(qkv_all_mm, 3)
            nc.scalar.activation(q_all, pe_hi[1][:], ACT.Identity, bias=bq).then_inc(qkv_all_out, 1)

            def exponents(b, h):
                wait(act, x_neg, b, h + 1)
                wait_head(act, xt_mm, b, h, back=4)
                for t in range(TILES):
                    nc.scalar.activation(p_x[:, h % 4, t, :], bank(HEAD_BANK[h])[:, SEQ * t:SEQ * t + SEQ], ACT.Exp,
                                         bias=xneg[:, h % 4, t:t + 1], scale=float(XDIM) ** -0.5).then_inc(x_exp.sem, 1)

            def copy_turned(b, h):
                wait(act, xt_mm, b, h + 1)
                wait_head(act, xo_mm, b, h, back=4)
                nc.scalar.copy(pT_x[:, h % 4], bank(4 + h % 2).rearrange("p (k q) -> p k q", k=TILES))\
                    .then_inc(xt_out.sem, 1)

            def square_out(b):
                wait(act, xcentred, b)
                nc.scalar.activation(centred2[:], centred[:], ACT.Square).then_inc(xsquared.sem, 1)

            def deviation_out(b):
                nc.scalar.preload_act_table(ACT.Sqrt)
                wait(act, xvar_mm, b)
                nc.scalar.activation(std[:], bank(LEND)[:, 0:SEQ], ACT.Sqrt, bias=eps[:, 0:1]).then_inc(xdeviated.sem, 1)
                nc.scalar.preload_act_table(ACT.Exp)

            def take_qk(n, i):
                t, part = FILLS[i]
                wait(act, qkv_mm, n, i + 1)
                if later(n):
                    wait(act, qkT_mm, n - 1, 2 * t + 2)
                nc.scalar.copy(raw[:, t, INNER * part:INNER * part + INNER], FILL[:]).then_inc(qkv_copied.sem, 1)

            def square_qk(n, i):
                t, part = FILLS[i]
                wait(act, qkv_mm, n, i + 1)
                if t:
                    wait(act, norm2_done, n, 1)
                elif later(n):
                    wait(act, norm2_done, n - 1)
                nc.scalar.activation(squares[:, INNER * part:INNER * part + INNER], FILL[:], ACT.Square)\
                    .then_inc(squared.sem, 1)

            def heads(b):
                for h in range(XHEADS):
                    run_head(copy_turned, b, h, 2)
                    run(exponents, b, h, steps=BATCH)
                    for at, stage in (10, square_out), (12, deviation_out):
                        if h == at:
                            run(stage, b - 1, steps=BATCH)
                    run_ahead(b, h, [(6, take_qk, 0), (6, square_qk, 0), (9, square_qk, 1), (9, take_qk, 1),
                                     (11, square_qk, 2), (11, take_qk, 2)])

            heads(0)
            with act.Fori(1, BATCH) as b:
                heads(b)
            heads(BATCH)

            def take_v(n, i):
                wait(act, qkv_mm, n, i + 1)
                if later(n):
                    wait(act, v_moved, n - 1)
                nc.scalar.copy(v_tok[:, FILLS[i][0], :], FILL[:]).then_inc(qkv_copied.sem, 1)

            def root(n, t):
                wait(act, norm2_done, n, t + 1)
                nc.scalar.activation(norm[:, t, :], norm2[:, t, :], ACT.Sqrt).then_inc(norm_done.sem, 1)

            def copy_qkT(n, t, part):
                wait(act, qkT_mm, n, 2 * t + part + 1)
                nc.scalar.copy(qkT[:, PAIRS * part:PAIRS * part + PAIRS, P * t:P * t + P],
                               pe_lo[t][:].rearrange("p (a s) -> p a s", a=PAIRS)).then_inc(qkT_out.sem, 1)

            def exponent(n, t):
                wait(act, shifted, n, t + 1)
                nc.scalar.activation(probs[:, t, :], probs[:, t, :], ACT.Exp, scale=QK_SCALE).then_inc(exp_done.sem, 1)

            def copy_probsT(n, t):
                wait(act, pT_mm, n, t + 1)
                nc.scalar.copy(probsT[:, t, :], pe_lo[t][:]).then_inc(pT_out.sem, 1)

            def copy_attT(n, half):
                wait(act, attT_mm, n, half + 1)
                nc.scalar.copy(attT[:, 4 * half:4 * half + 4, :],
                               pe_hi[1][:].rearrange("p (a s) -> p a s", a=4)).then_inc(attT_out.sem, 1)

            def square_centred(n):
                wait(act, centre_done, n)
                nc.scalar.activation(centred2[:], centred[:], ACT.Square).then_inc(csq_done.sem, 1)

            def deviation(n):
                wait(act, var_mm, n)
                nc.scalar.activation(std[:], bank(6)[:, 0:SEQ], ACT.Sqrt, bias=eps[:, 0:1]).then_inc(std_done.sem, 1)

            def table(n, function):
                nc.scalar.preload_act_table(function)

            def gates_of(n):
                for j, (f0, fs) in enumerate(CHUNKS):
                    wait(act, gate_mm, n, max(j, 1))
                    src = bank(7)[0:fs, SEQ * j:SEQ * j + SEQ] if j < 2 else bank(6)[0:fs, 0:SEQ]
                    nc.scalar.activation(gelu[0:fs, j, :], src, ACT.Gelu, bias=b_1[0:fs, 1, j:j + 1])\
                        .then_inc(gelu_done.sem, 1)

            def turn(n):
                run(table, n - 1, ACT.Exp)
                run(exponent, n - 1, 0)
                run(copy_qkT, n - 1, 1, 0)
                run(take_qk, n, 1)
                run(copy_qkT, n - 1, 1, 1)
                run(square_centred, n - 2)
                run(table, n, ACT.Sqrt)
                run(root, n, 0)
                run(deviation, n - 2)
                run(take_qk, n, 2)
                run(square_qk, n, 2)
                run(copy_probsT, n - 1, 0)
                run(take_qk, n, 3)
                run(table, n - 1, ACT.Exp)
                run(exponent, n - 1, 1)
                run(square_qk, n, 3)
                run(table, n - 2, ACT.Gelu)
                run(gates_of, n - 2)
                run(take_v, n, 4)
                run(copy_probsT, n - 1, 1)
                run(take_v, n, 5)
                run(copy_qkT, n, 0, 0)
                run(table, n, ACT.Sqrt)
                run(root, n, 1)
                run(copy_qkT, n, 0, 1)
                run(take_qk, n + 1, 0)
                run(square_qk, n + 1, 0)
                run(copy_attT, n - 1, 0)
                run(copy_attT, n - 1, 1)
                run(square_qk, n + 1, 1)

            for n in range(-1, 2):
                turn(n)
            with act.Fori(2, STEPS - 1) as n:
                turn(n)
            for n in range(STEPS - 1, STEPS + 2):
                turn(n)

            act.wait_ge(fin_mm, 1)
            nc.scalar.copy(x_in[:], pe_lo[0][:].rearrange("p (a d) -> p a d", a=BATCH * TILES)).then_inc(fin_copied, 1)

        @block.vector
        def _(dve):
            done = [0]

            def link(ins):
                done[0] += 1
                ins.then_inc(pre_dve, 1)
                dve.wait_ge(pre_dve, done[0])

            def per_token(a):
                return a[:].rearrange("p (i o) -> p i o", o=1).to_broadcast([P, BATCH * TILES, DIM])

            dve.wait_ge(x_loaded, 32)
            link(nc.vector.tensor_reduce(x_sum[:], x_in[:], AX.X, ALU.add))
            link(nc.vector.tensor_scalar(x_mean[:], x_sum[:], 1.0 / DIM, None, ALU.mult))
            link(nc.vector.tensor_tensor(x_centred, x_in[:], per_token(x_mean), ALU.subtract))
            assert done[0] == DVE_CENTRED
            link(nc.vector.memset(xs[64:P, 0:1], 0.0))
            link(nc.vector.memset(xfT[64:P, 0:1], 0.0))
            for buffer in (mask_top, ones_top):
                link(nc.vector.memset(buffer[:], 0.0))
            dve.wait_ge(pre_act, 1)
            link(nc.vector.tensor_reduce(x_var[:], x_squares, AX.X, ALU.add))
            dve.wait_ge(pre_act, 2)
            link(nc.vector.reciprocal(x_rstd[:], x_std[:]))
            link(nc.vector.tensor_tensor(x_normed, x_centred, per_token(x_rstd), ALU.mult))
            assert done[0] == DVE_NORMED
            dve.wait_ge(pre_pe, 1)
            link(nc.vector.tensor_copy(xT[:], pe_lo[0][:]))
            assert done[0] == DVE_XT
            dve.wait_ge(pre_pe, 2)
            link(nc.vector.tensor_copy(cT, pe_lo[1][:]))
            assert done[0] == DVE_CT
            dve.wait_ge(pre_pe, 3)
            link(nc.vector.tensor_copy(xnT, pe_hi[0][:]))
            assert done[0] == DVE_XNT
            dve.wait_ge(loaded, 16 * n_loads)
            link(nc.vector.tensor_copy(mask_top[0:1, :], mask_u8[:]))
            link(nc.vector.tensor_scalar(mask_top[0:1, :], mask_top[0:1, :], -1e30 * float(XDIM) ** 0.5, None, ALU.mult))
            link(nc.vector.memset(ones_top[0:1, :], 1.0))
            link(nc.vector.tensor_copy(ident_bf[:], ident[:]))
            for t in range(TILES):
                link(nc.vector.tensor_copy(window_mask[:, t], window_mask_f[:, t:t + 1, :].to_broadcast([P, 8, 64])))
            assert done[0] == DVE_ALL

            def values(b):
                if later(b):
                    wait(dve, xo_mm, b - 1)
                nc.vector.tensor_tensor(
                    v_aug[:, :, :, 0:XDIM], v_all[:, bass.ds(b * TILES, TILES)],
                    bv_row.rearrange("p (o h d) -> p o h d", o=1, d=XDIM).to_broadcast([P, TILES, XHEADS, XDIM]),
                    ALU.add).then_inc(xv_out.sem, 1)

            def maxima(b, h):
                wait(dve, xs_mm, b, h + 1)
                wait_head(dve, x_exp, b, h, back=4, each=2)
                nc.vector.tensor_reduce(xmax[:, h % 4, :], bank(HEAD_BANK[h]).rearrange("p (t k) -> p t k", t=TILES),
                                        AX.X, ALU.max).then_inc(x_max.sem, 1)
                wait(dve, x_max, b, h + 1)
                nc.vector.tensor_scalar(xneg[:, h % 4, :], xmax[:, h % 4, :], -float(XDIM) ** -0.5, None, ALU.mult)\
                    .then_inc(x_neg.sem, 1)

            def take_outputs(b, m):
                wait(dve, xo_mm, b, PER * (m + 1))
                if m:
                    wait(dve, xon_done, b, m)
                elif later(b):
                    wait(dve, xon_done, b - 1)
                nc.vector.tensor_copy(xo, bank(6 + m % 2)[:, 0:SEQ]).then_inc(xo_out.sem, 1)

            def scale_outputs(b, m):
                wait(dve, xsum_mm, b, m + 1)
                nc.vector.reciprocal(xrec, bank(6 + m % 2)[:, SEQ:2 * SEQ]).then_inc(xrec_done.sem, 1)
                wait(dve, xrec_done, b, m + 1)
                nc.vector.tensor_tensor(xon[:, m, :], xo, xrec, ALU.mult).then_inc(xon_done.sem, 1)

            def add_out(b):
                bs = bass.ds(b * SEQ, SEQ)
                wait(dve, xy_mm, b)
                nc.vector.tensor_scalar(xtmp, bank(LEND)[:, 0:SEQ], bxo[:, 0:1], tgate[:, 0:1], ALU.add, ALU.mult)\
                    .then_inc(xy_scaled.sem, 1)
                wait(dve, xy_scaled, b)
                nc.vector.tensor_tensor(x2T[:, bs], xtmp, xT[:, bs], ALU.add).then_inc(xy_done.sem, 1)

            def centre_out(b):
                wait(dve, xmean_mm, b)
                wait(dve, xy_done, b)
                nc.vector.tensor_tensor(centred[:], x2T[:, bass.ds(b * SEQ, SEQ)], bank(LEND)[:, 0:SEQ], ALU.subtract)\
                    .then_inc(xcentred.sem, 1)

            def norm_out(b):
                wait(dve, xdeviated, b)
                nc.vector.reciprocal(rstd[:], std[:]).then_inc(xinverted.sem, 1)
                wait(dve, xcentred, b)
                wait(dve, xinverted, b)
                nc.vector.tensor_tensor(xT[:, bass.ds(b * SEQ, SEQ)], centred[:], rstd[:], ALU.mult)\
                    .then_inc(x_ready.sem, 1)

            def lengths(n, t):
                wait(dve, squared, n, 2 * t + 2)
                nc.vector.tensor_reduce(norm2[:, t, :], squares[:].rearrange("p (h d) -> p h d", d=HDIM), AX.X, ALU.add)\
                    .then_inc(norm2_done.sem, 1)

            def sines(n, t):
                layer = n // BATCH
                wait(dve, qkv_copied, n, 2 * t + 2)
                if t:
                    wait(dve, qk_done, n, 1)
                elif later(n):
                    wait(dve, qk_done, n - 1)
                sine_half(nc.vector, n, t, 1).then_inc(sin_done.sem, 1)

            def heads(b):
                for h in range(XHEADS):
                    if h == 4:
                        run(values, b, steps=BATCH)
                    run_group(take_outputs, b, h, 5)
                    for at, stage in (8, add_out), (10, centre_out):
                        if h == at:
                            run(stage, b - 1, steps=BATCH)
                    run(maxima, b, h, steps=BATCH)
                    if h == 14:
                        run(norm_out, b - 1, steps=BATCH)
                    run_group(scale_outputs, b, h, 6)
                    run_ahead(b, h, [(10, lengths, 0), (10, sines, 0)])

            heads(0)
            with dve.Fori(1, BATCH) as b:
                heads(b)
            dve.wait_ge(pre_pool, POOL_ALL)
            heads(BATCH)

            def inverses(n, t):
                wait(dve, norm_done, n, t + 1)
                nc.vector.tensor_scalar(norm_c[:, t, :], norm[:, t, :], 1e-12, None, ALU.max).then_inc(normc_done.sem, 1)
                wait(dve, normc_done, n, t + 1)
                nc.vector.reciprocal(inv_norm[:, t, :], norm_c[:, t, :]).then_inc(inv_done.sem, 1)

            def rotate(n, t):
                wait(dve, sin_done, n, t + 1)
                wait(dve, swung, n, t + 1)
                wait(dve, cos_done, n, t + 1)
                nc.vector.tensor_tensor(by_sin[:], by_sin[:], by_cos[:], ALU.add).then_inc(rot_done.sem, 1)
                wait(dve, rot_done, n, t + 1)
                wait(dve, inv_done, n, t + 1)
                nc.vector.tensor_tensor(
                    raw[:, t, :].rearrange("p (h d) -> p h d", d=HDIM), by_sin[:].rearrange("p (h d) -> p h d", d=HDIM),
                    inv_norm[:, t, :].rearrange("p (h o) -> p h o", o=1).to_broadcast([P, 2 * HEADS, HDIM]), ALU.mult)\
                    .then_inc(qk_done.sem, 1)

            def heads_split(ap):
                return ap.rearrange("p (a o d) -> p o a d", o=2, d=64)

            def shift(n, t):
                wait(dve, s_mm, n, t + 1)
                ps = pe_lo[t][:].rearrange("p (o a d) -> p o a d", o=2, d=64)
                nc.vector.tensor_reduce(row_max[:, t, :], pe_lo[t][:].rearrange("p (h d) -> p h d", d=64), AX.X, ALU.max)\
                    .then_inc(max_done.sem, 1)
                wait(dve, max_done, n, t + 1)
                nc.vector.tensor_tensor(
                    heads_split(probs[:, t, :]), ps,
                    row_max[:, t, :].rearrange("p (o a d) -> p o a d", o=2, d=1).to_broadcast([P, 2, PAIRS, 64]),
                    ALU.subtract).then_inc(shifted.sem, 1)

            def sums(n, t):
                wait(dve, exp_done, n, t + 1)
                nc.vector.tensor_reduce(row_sum[:, t, :], probs[:, t, :].rearrange("p (h d) -> p h d", d=64), AX.X, ALU.add)\
                    .then_inc(sum_done.sem, 1)
                wait(dve, sum_done, n, t + 1)
                nc.vector.reciprocal(row_inv[:, t, :], row_sum[:, t, :]).then_inc(rinv_done.sem, 1)

            def take_att(n, t):
                wait(dve, pv_mm, n, t + 1)
                wait(dve, rinv_done, n, t + 1)
                nc.vector.tensor_tensor(
                    heads_split(att[:, t, :]), pe_lo[t][:].rearrange("p (o a d) -> p o a d", o=2, d=64),
                    row_inv[:, t, :].rearrange("p (a o d) -> p o a d", o=2, d=1).to_broadcast([P, 2, PAIRS, 64]),
                    ALU.mult).then_inc(att_done.sem, 1)

            def add_x(n):
                x0 = (n % BATCH) * SEQ
                wait(dve, y_mm, n)
                nc.vector.tensor_tensor(xfT[0:64, :], xT[0:64, bass.ds(x0, SEQ)], bank(6)[0:64, 0:SEQ], ALU.add)\
                    .then_inc(x1_done.sem, 1)
                nc.vector.tensor_tensor(xfT[64:P, 1:SEQ], xT[64:P, bass.ds(x0, SEQ - 1)], bank(6)[64:P, 0:SEQ - 1], ALU.add)\
                    .then_inc(x1_done.sem, 1)
                nc.vector.tensor_tensor(x1T[:], xT[:, bass.ds(x0, SEQ)], bank(6)[:, 0:SEQ], ALU.add)\
                    .then_inc(x1_done.sem, 1)

            def centre(n):
                wait(dve, mean_mm, n)
                wait(dve, x1_done, n)
                nc.vector.tensor_tensor(centred[:], xfT[:], bank(7)[:, 0:SEQ], ALU.subtract).then_inc(centre_done.sem, 1)

            def scale_norm(n):
                wait(dve, std_done, n)
                nc.vector.reciprocal(rstd[:], std[:]).then_inc(rstd_done.sem, 1)
                wait(dve, centre_done, n)
                wait(dve, rstd_done, n)
                nc.vector.tensor_tensor(normed[:], centred[:], rstd[:], ALU.mult).then_inc(normed_done.sem, 1)
                wait(dve, normed_done, n)
                dve.wait_ge(small_loaded, (n // BATCH + 1) * (16 * SMALLS))
                nc.vector.tensor_scalar(ffn_in[:], normed[:], ln_gb[:, 0:1], ln_gb[:, 1:2], ALU.mult, ALU.add)\
                    .then_inc(ffnin_done.sem, 1)

            def inner(n):
                wait(dve, up_mm, n)
                for j, (f0, fs) in enumerate(CHUNKS):
                    src = bank(7)[0:fs, SEQ * j:SEQ * j + SEQ] if j < 2 else bank(6)[0:fs, 0:SEQ]
                    nc.vector.scalar_tensor_tensor(hidden[0:fs, j, :], src, b_1[0:fs, 0, j:j + 1], gelu[0:fs, j, :],
                                                   ALU.add, ALU.mult).then_inc(hid_done.sem, 1)

            def new_x(n):
                x0 = (n % BATCH) * SEQ
                wait(dve, down_mm, n)
                nc.vector.scalar_tensor_tensor(xT[:, bass.ds(x0, SEQ)], bank(7)[:, 0:SEQ], b_2[:, 0:1], x1T[:],
                                               ALU.add, ALU.add).then_inc(x_ready.sem, 1)

            def turn(n):
                run(inverses, n, 1)
                run(take_att, n - 1, 1)
                run(new_x, n - 2)
                run(rotate, n, 1)
                run(shift, n, 0)
                run(lengths, n + 1, 0)
                run(sums, n, 0)
                run(add_x, n - 1)
                run(centre, n - 1)
                run(sines, n + 1, 0)
                run(scale_norm, n - 1)
                run(inverses, n + 1, 0)
                run(shift, n, 1)
                run(rotate, n + 1, 0)
                run(take_att, n, 0)
                run(lengths, n + 1, 1)
                run(inner, n - 1)
                run(sums, n, 1)
                run(sines, n + 1, 1)

            for n in range(-1, 2):
                turn(n)
            with dve.Fori(2, STEPS - 1) as n:
                turn(n)
            for n in range(STEPS - 1, STEPS + 2):
                turn(n)

            wait(dve, x_ready, STEPS - 1)
            nc.vector.scalar_tensor_tensor(x2T[:], xT[:], tgate[:, 1:2], x2T[:], ALU.mult, ALU.add).then_inc(fin_done, 1)


def _laid_out(i):
    import numpy as np

    f32 = np.float32

    def by_group(a, axis):
        shape = a.shape[:axis] + (XHEADS, GROUP) + a.shape[axis + 1:]
        spread = np.zeros(shape, f32)
        at = (slice(None),) * axis + (slice(None), slice(0, XDIM))
        spread[at] = a.reshape(a.shape[:axis] + (XHEADS, XDIM) + a.shape[axis + 1:])
        return spread

    def by_chunk(a):
        padded = np.zeros(a.shape[:1] + (len(CHUNKS) * P,) + a.shape[2:], f32)
        padded[:, 0:FFN] = a
        return padded

    xcolumns = np.stack([i["L0_xattn_bq"], i["L0_xattn_bk"], i["L0_xattn_bo"]], 1)
    b1 = i["L0_ffn_b1"]
    columns = np.concatenate([by_chunk(b1[:, 0:FFN]).reshape(DEPTH, len(CHUNKS), P),
                              by_chunk(b1[:, FFN:]).reshape(DEPTH, len(CHUNKS), P),
                              i["L0_ffn_ln_g"].reshape(DEPTH, 1, P), i["L0_ffn_ln_b"].reshape(DEPTH, 1, P),
                              i["L0_ffn_b2"].reshape(DEPTH, 1, P)], 1).transpose(0, 2, 1)
    return {
        "x": i["x"], "ctx": i["ctx_1024"], "mask": i["mask_BxS2_bf0"],
        "g_xattn": i["g_xattn"], "g_ffn": i["g_ffn"],
        "Wq": i["L0_xattn_Wq"], "Wk": i["L0_xattn_Wk"], "Wv": i["L0_xattn_Wv"],
        "Wxo": by_group(i["L0_xattn_Wo"], 0).reshape(MGROUPS, P, DIM).transpose(1, 0, 2),
        "bv": i["L0_xattn_bv"], "xcolumns": xcolumns,
        "Wqkv": i["L0_ffn_Wqkv"], "q_scale": i["L0_ffn_q_scale"], "k_scale": i["L0_ffn_k_scale"],
        "Wo": i["L0_ffn_Wo"], "W1": i["L0_ffn_W1"], "W2": by_chunk(i["L0_ffn_W2"]), "columns": columns,
    }


def _shape_tables():
    import numpy as np

    f32 = np.float32
    half = np.arange(0, HDIM, 2, dtype=f32)
    t = np.arange(SEQ, dtype=f32)
    freqs = t[:, None] * (f32(1.0) / f32(10000.0) ** (half / f32(HDIM)))[None, :]
    scale = ((half + f32(0.4 * HDIM)) / f32(1.4 * HDIM))[None, :] ** ((t - SEQ // 2) / f32(WIN // 2))[:, None]
    two = lambda a: np.concatenate([a, a], -1)
    cos, sin, scale = two(np.cos(freqs)), np.concatenate([-np.sin(freqs), np.sin(freqs)], -1), two(scale)
    a, j = np.arange(WIN)[:, None], np.arange(2 * WIN)[None, :]
    seen = np.where(j < WIN, j >= a, j - WIN <= a)
    hidden = np.tile(np.where(seen, 0.0, -1e30), (WINDOWS, 1))
    hidden[:WIN, :WIN] = -1e30
    p = np.arange(P)
    ones_row = (p % GROUP == XDIM).astype(f32)
    return {
        "t_cos": np.concatenate([cos * scale, cos / scale], -1).astype(f32),
        "t_sin": np.concatenate([sin * scale, sin / scale], -1).astype(f32),
        "t_mask": hidden.astype(f32),
        "t_ident": np.eye(P, dtype=f32),
        "t_spread": ((p[:, None] // GROUP == p[None, :] // GROUP) * ones_row[:, None]).astype(f32),
        "t_headrows": (p[:, None] // XDIM == np.arange(XHEADS)[None, :]).astype(f32),
    }


def kernel(**inputs):
    import numpy as _np
    import concourse.bacc as _bacc
    from concourse import mybir as _mybir
    from concourse.bass_utils import run_bass_kernel_spmd as _run

    nc = _bacc.Bacc("TRN2", target_bir_lowering=False, num_devices=1)
    arrays, args = {}, []
    given = _laid_out({name: _np.asarray(a) for name, a in inputs.items()}) | _shape_tables()
    for name, a in given.items():
        arrays[f"in_{name}_dram"] = a = _np.ascontiguousarray(a)
        args.append(nc.dram_tensor(f"in_{name}_dram", a.shape, _mybir.dt.from_np(a.dtype), kind="ExternalInput").ap())
    out = nc.dram_tensor("out_0_dram", (BATCH, SEQ, DIM), _mybir.dt.float32, kind="ExternalOutput").ap()
    build(nc, *args, out)
    r = _run(nc, [arrays], core_ids=[0])
    return r.results[0]["out_0_dram"]
```
